# Optimizing a Trainium2 kernel written in Bass

```python
import numpy as np
import jax
import jax.numpy as jnp

def _softmax(x, axis=-1):
    return jax.nn.softmax(x, axis=axis)

def _gelu(x):
    return jax.nn.gelu(x, approximate=True)

def _silu(x):
    return jax.nn.silu(x)

def _sigmoid(x):
    return jax.nn.sigmoid(x)

def _layernorm(x, axis=-1, eps=1e-05):
    m = jnp.mean(x, axis=axis, keepdims=True)
    v = jnp.var(x, axis=axis, keepdims=True)
    return (x - m) / jnp.sqrt(v + eps)

def _scatter_add(tgt, idx, src, axis=0):
    return tgt.at[idx].add(src)

def _segment_sum(src, seg, n):
    return jax.ops.segment_sum(src, seg, n)
kernel_name = 'mk_flamingo_gated_d1_seqx_r8_e96fe5'

def setup_inputs(seed: int=0):
    np.random.seed(seed)
    _w = jnp.asarray

    def _rec_inputs():
        import jax
        import jax.numpy as jnp
        _rk = jax.random.key(seed)
        x = -0.0003929 + 0.9999 * jax.random.normal(jax.random.fold_in(_rk, 1), (16, 64, 512), jnp.float32)
        _lenS = 64 - jax.random.randint(jax.random.fold_in(_rk, 7), (16,), 0, max(1, 64 // 4) + 1, jnp.int32)
        _lenS2 = 64 - jax.random.randint(jax.random.fold_in(_rk, 8), (16,), 0, max(1, 64 // 4) + 1, jnp.int32)
        _ctx_1024P = jax.random.normal(jax.random.fold_in(_rk, 11), (16, 16, 128), jnp.float32)
        _ctx_1024c = jax.random.dirichlet(jax.random.fold_in(_rk, 511), 0.3 * jnp.ones((16,), jnp.float32), (16, 64))
        _ctx_1024t = jnp.einsum('bsk,bkd->bsd', _ctx_1024c, _ctx_1024P)
        _ctx_1024t = _ctx_1024t * jax.lax.rsqrt(jnp.mean(jnp.square(_ctx_1024t)) + 1e-12) * 0.953939
        ctx_1024 = -1.39393e-06 + 0.999914 * (_ctx_1024t + 0.3 * jax.random.normal(jax.random.fold_in(_rk, 611), (16, 64, 128), jnp.float32))
        _g = jax.random.normal(jax.random.fold_in(_rk, 9001), (2, 1), jnp.float32)
        _g = jnp.sign(_g) * jnp.maximum(jnp.abs(_g), 1.0) + (_g == 0) * 1.0
        g_xattn = _g[0]
        g_ffn = _g[1]
        return (x, ctx_1024, g_xattn, g_ffn)
    x, ctx_1024, g_xattn, g_ffn = _rec_inputs()

    def _L0_xattn_setup():
        import jax, jax.numpy as jnp
        import numpy as np
        import math
        DIM_V = 64
        key = jax.random.key(seed)
        k1, k2, k3, k4, k5, k6 = jax.random.split(key, 6)
        B, C, N, M = (8, DIM_V, 512, 128)
        pcd_up = jax.random.normal(k1, (B, C, N), dtype=jnp.float32)
        pcd_down = jax.random.normal(k2, (B, C, M), dtype=jnp.float32)
        s = 1.0 / math.sqrt(C)
        Wq = jax.random.normal(k3, (C, C), dtype=jnp.float32) * s
        Wk = jax.random.normal(k4, (C, C), dtype=jnp.float32) * s
        Wv = jax.random.normal(k5, (C, C), dtype=jnp.float32) * s
        Wskip = jax.random.normal(k6, (C, C), dtype=jnp.float32) * s
        return {'pcd_up': pcd_up, 'pcd_down': pcd_down, 'Wq': Wq, 'Wk': Wk, 'Wv': Wv, 'Wskip': Wskip}
    _L0_xattn_all = _L0_xattn_setup()
    _L0_xattn_in = {k: v for k, v in _L0_xattn_all.items() if k in ('Wq', 'Wk', 'Wv', 'Wskip')}
    del _L0_xattn_all

    def _L0_ffn_setup():
        import jax, jax.numpy as jnp
        import numpy as np
        DIM = 512
        INTER = 1792
        SPARSITY = 32
        RANK = 16
        key = jax.random.key(seed)
        ks = jax.random.split(key, 5)
        B, T = (32, 1)
        x = jax.random.normal(ks[0], (B, T, DIM), dtype=jnp.float32)
        c1_w = jax.random.normal(ks[1], (RANK, DIM), dtype=jnp.float32) * (1.0 / np.sqrt(DIM))
        c2_w = jax.random.normal(ks[2], (INTER, RANK), dtype=jnp.float32) * (1.0 / np.sqrt(RANK))
        w1 = jax.random.normal(ks[3], (INTER, DIM), dtype=jnp.float32) * (1.0 / np.sqrt(DIM))
        w2t = jax.random.normal(ks[4], (INTER, DIM), dtype=jnp.float32) * (1.0 / np.sqrt(INTER))
        return {'x': x, 'c1_w': c1_w, 'c2_w': c2_w, 'w1': w1, 'w2t': w2t}
    _L0_ffn_all = _L0_ffn_setup()
    _L0_ffn_in = {k: v for k, v in _L0_ffn_all.items() if k in ('c1_w', 'c2_w', 'w1', 'w2t')}
    del _L0_ffn_all
    return {'x': x, 'ctx_1024': ctx_1024, 'g_xattn': g_xattn, 'g_ffn': g_ffn, 'L0_xattn_Wq': _L0_xattn_in['Wq'], 'L0_xattn_Wk': _L0_xattn_in['Wk'], 'L0_xattn_Wv': _L0_xattn_in['Wv'], 'L0_xattn_Wskip': _L0_xattn_in['Wskip'], 'L0_ffn_c1_w': _L0_ffn_in['c1_w'], 'L0_ffn_c2_w': _L0_ffn_in['c2_w'], 'L0_ffn_w1': _L0_ffn_in['w1'], 'L0_ffn_w2t': _L0_ffn_in['w2t']}

def reference(x, ctx_1024, g_xattn, g_ffn, L0_xattn_Wq, L0_xattn_Wk, L0_xattn_Wv, L0_xattn_Wskip, L0_ffn_c1_w, L0_ffn_c2_w, L0_ffn_w1, L0_ffn_w2t):
    import jax
    import jax.numpy as jnp

    def _L0_xattn_ref(pcd_up, pcd_down, Wq, Wk, Wv, Wskip):
        import jax, jax.numpy as jnp
        import numpy as np
        import math
        DIM_V = 64
        q = jnp.einsum('oc,bcn->bon', Wq, pcd_up)
        k = jnp.einsum('oc,bcm->bom', Wk, pcd_down)
        v = jnp.einsum('oc,bcm->bom', Wv, pcd_down)
        C = q.shape[1]
        scale = jnp.sqrt(jnp.asarray(C, dtype=q.dtype))
        energy = jnp.einsum('bcn,bcm->bnm', q, k) / scale
        attention = jax.nn.softmax(energy, axis=-1)
        x = jnp.einsum('bnm,bcm->bcn', attention, v)
        skip = jnp.einsum('oc,bcn->bon', Wskip, pcd_up)
        return skip + x

    def _L0_ffn_ref(x, c1_w, c2_w, w1, w2t):
        import jax, jax.numpy as jnp
        import numpy as np
        DIM = 512
        INTER = 1792
        SPARSITY = 32
        RANK = 16
        B, T, M = x.shape
        xf = x.reshape(B * T, M)
        inter = xf @ c1_w.T @ c2_w.T
        n_blocks = INTER // SPARSITY
        blk = inter.reshape(B * T, n_blocks, SPARSITY)
        idx = jnp.argmax(blk, axis=-1) + jnp.arange(0, INTER, SPARSITY)
        w1_g = w1[idx]
        w2_g = w2t[idx]
        h = jax.nn.relu(jnp.einsum('bkm,bm->bk', w1_g, xf))
        out = jnp.einsum('bk,bkm->bm', h, w2_g)
        return out.reshape(B, T, M)
    x = x + jnp.tanh(g_xattn[0]) * _L0_xattn_ref(_layernorm(x, axis=-1), ctx_1024, L0_xattn_Wq, L0_xattn_Wk, L0_xattn_Wv, L0_xattn_Wskip)
    x = x + jnp.tanh(g_ffn[0]) * _L0_ffn_ref(_layernorm(x, axis=-1), L0_ffn_c1_w, L0_ffn_c2_w, L0_ffn_w1, L0_ffn_w2t)
    return x

_drawn_inputs = setup_inputs


def setup_inputs(seed=0):
    import zlib

    import numpy as np

    out = dict(_drawn_inputs(seed))
    spreads = {}
    factors = {}
    for name, (base, spread) in spreads.items():
        noise = np.random.default_rng([zlib.crc32(name.encode()), seed]).standard_normal(out[name].shape)
        drawn = base * np.exp(spread * noise) if base else spread * noise
        out[name] = jnp.asarray(drawn.astype(out[name].dtype))
    for name, factor in factors.items():
        out[name] = (out[name] * factor).astype(out[name].dtype)
    return out
```

```python
import concourse.bass as bass
from concourse import mybir
from contextlib import ExitStack


def flamingo_gated_layer(
    nc: bass.Bass,
    x: bass.AP,
    ctx: bass.AP,
    g_xattn: bass.AP,
    g_ffn: bass.AP,
    Wq: bass.AP,
    Wk: bass.AP,
    Wv: bass.AP,
    Wskip: bass.AP,
    c1_w: bass.AP,
    c2_w: bass.AP,
    w1: bass.AP,
    w2t: bass.AP,
    out: bass.AP,
):
    f32 = mybir.dt.float32
    f32r = mybir.dt.float32r
    bf16 = mybir.dt.bfloat16
    ALU = mybir.AluOpType
    ACT = mybir.ActivationFunctionType
    AX = mybir.AxisListType

    P = 128
    B, C, N = x.shape
    M = ctx.shape[2]
    R = c1_w.shape[0]
    F = w1.shape[0]
    BLK = 32
    TILES = B * C // P
    PAIR = P // C
    ND = N // P
    NF = F // P
    GF = 4
    GROUPS = [(g, min(GF, NF - g)) for g in range(0, NF, GF)]
    NG = len(GROUPS)
    GW = GF * P
    EPS = 1e-5
    REP = P // R

    x_rows = x.rearrange("(t b) c n -> (b c) t n", b=PAIR)
    out_rows = out.rearrange("(t b) c n -> (b c) t n", b=PAIR)
    ctx_rows = ctx.rearrange("(t b) c m -> (b c) t m", b=PAIR)
    w1_rows = w1.rearrange("(k p) n -> p k n", p=P)
    w2_rows = w2t.rearrange("(k p) n -> p k n", p=P)
    c2_rows = c2_w.rearrange("(k p) r -> p k r", p=P)

    stack = ExitStack()
    with stack:
        def sb(name, shape, dt=f32):
            return stack.enter_context(nc.sbuf_tensor(name, shape, dt))

        def bank(name):
            return stack.enter_context(nc.psum_tensor(name, [P, 512], f32))

        def sem(name):
            return stack.enter_context(nc.semaphore(name))

        w1T_hi = sb("w1T_hi", [P, ND, F], f32r)
        w1T_lo = sb("w1T_lo", [P, ND, F], f32r)
        w2_hi = sb("w2_hi", [P, NF, N], f32r)
        w2_lo = sb("w2_lo", [P, NF, N], f32r)
        c2T = sb("c2T", [P, F], f32r)
        c1T_hi = sb("c1T_hi", [P, ND * P], f32r)
        c1T_lo = sb("c1T_lo", [P, ND * P], f32r)
        G_hi = sb("G_hi", [P, P], f32r)
        G_lo = sb("G_lo", [P, P], f32r)
        WT_hi = sb("WT_hi", [P, 2, P], f32r)
        WT_lo = sb("WT_lo", [P, 2, P], f32r)
        ident = sb("ident", [P, P])
        doubling = sb("doubling", [P, GW], bf16)
        minus_half = sb("minus_half", [P, 1])
        eps = sb("eps", [P, 1])
        gates = sb("gates", [P, 2])
        tanh_g = sb("tanh_g", [P, 2])
        W_bd = sb("W_bd", [P, 4, P])
        c2_raw = sb("c2_raw", [P, NF, R])
        c2_top = sb("c2_top", [P, NF, R], f32r)
        c2_parts = sb("c2_parts", [P, NF + 1, 4, R])
        w2_stage = sb("w2_stage", [P, 2, N])
        rows = sb("rows", [P, TILES, N])
        stats1 = sb("stats1", [P, 6])
        mv1 = sb("mv1", [P, 2])
        rstd1 = sb("rstd1", [P, 1])
        up = sb("up", [P, N])
        up_hi = sb("up_hi", [P, N], f32r)
        up_lo = sb("up_lo", [P, N], f32r)
        ctx_all = sb("ctx_all", [P, TILES, M])
        ctx_hi = sb("ctx_hi", [P, PAIR * M], f32r)
        ctx_lo = sb("ctx_lo", [P, PAIR * M], f32r)
        AV_hi = sb("AV_hi", [P, 4, P], f32r)
        AV_lo = sb("AV_lo", [P, 4, P], f32r)
        neg_max = sb("neg_max", [P, ND * PAIR])
        row_sum = sb("row_sum", [P, ND * PAIR])
        inv_sum = sb("inv_sum", [P, ND * PAIR])
        probs = sb("probs", [P, ND, PAIR, M])
        PT_hi = sb("PT_hi", [P, PAIR, N], f32r)
        PT_lo = sb("PT_lo", [P, PAIR, N], f32r)
        stats2 = sb("stats2", [P, 6])
        mv2 = sb("mv2", [P, 2])
        rstd2 = sb("rstd2", [P, 1])
        xf = sb("xf", [P, N])
        xfT_hi = sb("xfT_hi", [P, ND, P], f32r)
        xfT_lo = sb("xfT_lo", [P, ND, P], f32r)
        t_parts = sb("t_parts", [P, P], f32r)
        blk_max = sb("blk_max", [P, GW // BLK])
        is_max = sb("is_max", [P, GW], bf16)
        first = sb("first", [P, 2, GW], bf16)
        h = sb("h", [P, 2, GW])
        hT_hi = sb("hT_hi", [P, 2, GW], f32r)
        hT_lo = sb("hT_lo", [P, 2, GW], f32r)
        c1_rep = xf
        w1_stage = h

        inter_ps = [bank("inter0"), bank("inter1")]
        H_ps = [bank("H0"), bank("H1")]
        turn_ps = bank("turn")
        ffn_ps = bank("ffn")
        att_ps = [bank("att0"), bank("att1")]

        s_x = [sem("x0_in"), sem("xrest_in")]
        s_small = sem("small_in")
        s_c = sem("c_in")
        s_ctx = sem("ctx_in")
        s_w1 = [sem("w1_even_in"), sem("w1_odd_in")]
        s_w2 = [sem("w2_even_in"), sem("w2_odd_in")]
        s_out = sem("out_written")
        zeroed = sem("zeroed")
        ident_ready = sem("ident_ready")
        consts_ready = sem("consts_ready")
        tanh_ready = sem("tanh_ready")
        wprod_ready = sem("wprod_ready")
        whi_ready = sem("whi_ready")
        wlo_ready = sem("wlo_ready")
        w1_turned = sem("w1_turned")
        w1_hi_ready = sem("w1_hi_ready")
        w1_lo_ready = sem("w1_lo_ready")
        w2_hi_ready = sem("w2_hi_ready")
        w2_lo_ready = sem("w2_lo_ready")
        c1_turned = sem("c1_turned")
        c1_hi_ready = sem("c1_hi_ready")
        c1_lo_ready = sem("c1_lo_ready")
        c2_top_ready = sem("c2_top_ready")
        c2_parts_ready = sem("c2_parts_ready")
        c2_turned = sem("c2_turned")
        c2_ready = sem("c2_ready")
        consts2_ready = sem("consts2_ready")

        stats1_ready = sem("stats1_ready")
        mv1_ready = sem("mv1_ready")
        rstd1_ready = sem("rstd1_ready")
        up_ready = sem("up_ready")
        up_hi_ready = sem("up_hi_ready")
        up_lo_ready = sem("up_lo_ready")
        ctx_hi_ready = sem("ctx_hi_ready")
        ctx_lo_ready = sem("ctx_lo_ready")
        AV_done = sem("AV_done")
        AV_hi_ready = sem("AV_hi_ready")
        AV_lo_ready = sem("AV_lo_ready")
        energy_done = sem("energy_done")
        neg_max_ready = sem("neg_max_ready")
        exp_ready = sem("exp_ready")
        inv_sum_ready = sem("inv_sum_ready")
        probs_ready = sem("probs_ready")
        probs_turned = sem("probs_turned")
        PT_hi_ready = sem("PT_hi_ready")
        PT_lo_ready = sem("PT_lo_ready")
        xattn_done = sem("xattn_done")
        x2_ready = sem("x2_ready")
        stats2_ready = sem("stats2_ready")
        mv2_ready = sem("mv2_ready")
        var1_ready = sem("var1_ready")
        var2_ready = sem("var2_ready")
        rstd2_ready = sem("rstd2_ready")
        xf_ready = sem("xf_ready")
        xf_turned = sem("xf_turned")
        xfT_hi_ready = sem("xfT_hi_ready")
        xfT_lo_ready = sem("xfT_lo_ready")
        t_done = sem("t_done")
        t_hi_ready = sem("t_hi_ready")
        t_ready = sem("t_ready")
        inter_done = sem("inter_done")
        blk_max_ready = sem("blk_max_ready")
        is_max_ready = sem("is_max_ready")
        first_ready = sem("first_ready")
        H_done = sem("H_done")
        h_ready = sem("h_ready")
        h_turned = sem("h_turned")
        hT_hi_ready = sem("hT_hi_ready")
        hT_lo_ready = sem("hT_lo_ready")
        ffn_done = sem("ffn_done")
        out_ready = sem("out_ready")

        def wait_past(eng, semaphore, n):
            if not isinstance(n, int) or n > 0:
                eng.wait_ge(semaphore, n)

        def flat(buf):
            return buf[:].rearrange("p a b -> p (a b)")

        def chunks(ps):
            return ps[:].rearrange("p (d f) -> p d f", d=ND)

        def at_tile(buf, t):
            return buf[:, bass.ds(t, 1), :].rearrange("p o w -> p (o w)")

        def three_passes(ps, lhs_hi, lhs_lo, rhs_hi, rhs_lo, start=True, stop=True):
            nc.tensor.matmul(ps, lhs_hi, rhs_hi, start=start, stop=False)
            nc.tensor.matmul(ps, lhs_hi, rhs_lo, start=False, stop=False)
            return nc.tensor.matmul(ps, lhs_lo, rhs_hi, start=False, stop=stop)

        block = stack.enter_context(nc.Block())

        @block.sync
        def _(sp):
            sp.dma_start(rows[:, 0, :], x_rows[:, 0, :]).then_inc(s_x[0], 16)
            sp.wait_ge(zeroed, 1)
            for n, w in enumerate((Wk, Wq, Wv, Wskip)):
                for b in range(PAIR):
                    sp.dma_start(W_bd[b * C:(b + 1) * C, n, b * C:(b + 1) * C], w).then_inc(s_small, 16)
            sp.dma_start(ctx_all[:], ctx_rows).then_inc(s_ctx, 16)

            def load_w1(k, slot):
                sp.dma_start(w1_stage[:, slot, :], w1_rows[:, bass.ds(k, 1), :].rearrange("p o n -> p (o n)")
                             ).then_inc(s_w1[slot], 16)

            def load_w2(k, slot):
                sp.dma_start(w2_stage[:, slot, :], w2_rows[:, bass.ds(k, 1), :].rearrange("p o n -> p (o n)")
                             ).then_inc(s_w2[slot], 16)

            for slot in range(2):
                load_w1(slot, slot)
            for slot in range(2):
                load_w2(slot, slot)
            sp.dma_start(rows[:, 1:, :], x_rows[:, 1:, :]).then_inc(s_x[1], 16)
            with sp.Fori(1, NF // 2) as i:
                for slot in range(2):
                    sp.wait_ge(w1_turned, i * 2 + slot - 1)
                    load_w1(i * 2 + slot, slot)
                for slot in range(2):
                    sp.wait_ge(w2_lo_ready, i * 2 + slot - 1)
                    load_w2(i * 2 + slot, slot)
            with sp.Fori(0, TILES) as t:
                sp.wait_ge(out_ready, t + 1)
                sp.dma_start(out_rows[:, bass.ds(t, 1), :], rows[:, bass.ds(t, 1), :]).then_inc(s_out, 16)
            sp.wait_ge(s_out, 16 * TILES)

        @block.gpsimd
        def _(pool):
            nc.gpsimd.memset(W_bd[:], 0.0).then_inc(zeroed, 1)
            nc.gpsimd.memset(ident[:], 0.0).then_inc(zeroed, 1)
            nc.gpsimd.memset(minus_half[:], -0.5).then_inc(consts_ready, 1)
            nc.gpsimd.memset(eps[:], EPS).then_inc(consts_ready, 1)
            nc.gpsimd.memset(ctx_hi[:].bitcast(f32), 0.0).then_inc(consts_ready, 1)
            nc.gpsimd.memset(ctx_lo[:].bitcast(f32), 0.0).then_inc(consts_ready, 1)
            nc.gpsimd.memset(c2_parts[:, NF, :, :], 0.0).then_inc(consts_ready, 1)
            pool.wait_ge(zeroed, 2)
            nc.gpsimd.affine_select(out=ident[:], in_=ident[:], compare_op=ALU.not_equal, fill=1.0, base=0,
                                    pattern=[[-1, P]], channel_multiplier=1).then_inc(ident_ready, 1)

            def rstd1_step(t):
                pool.wait_ge(mv1_ready, t + 1)
                nc.gpsimd.tensor_tensor(rstd1[:], mv1[:, 1:2], eps[:], ALU.add).then_inc(var1_ready, 1)
                pool.wait_ge(var1_ready, t + 1)
                nc.gpsimd.tensor_tensor(rstd1[:], rstd1[:], minus_half[:], ALU.pow).then_inc(rstd1_ready, 1)

            def rstd2_step(t):
                pool.wait_ge(mv2_ready, t + 1)
                nc.gpsimd.tensor_tensor(rstd2[:], mv2[:, 1:2], eps[:], ALU.add).then_inc(var2_ready, 1)
                pool.wait_ge(var2_ready, t + 1)
                nc.gpsimd.tensor_tensor(rstd2[:], rstd2[:], minus_half[:], ALU.pow).then_inc(rstd2_ready, 1)

            def up_low(t):
                pool.wait_ge(up_hi_ready, t + 1)
                nc.gpsimd.tensor_tensor(up_lo[:], up[:], up_hi[:].bitcast(f32), ALU.subtract).then_inc(up_lo_ready, 1)

            def normalise(t):
                for half in range(2):
                    pool.wait_ge(inv_sum_ready, t * 2 + half + 1)
                    js = slice(half * ND // 2, (half + 1) * ND // 2)
                    cols = slice(half * ND * PAIR // 2, (half + 1) * ND * PAIR // 2)
                    pr = probs[:, js, :, :].rearrange("p j b m -> p (j b) m")
                    nc.gpsimd.tensor_tensor(pr, pr, inv_sum[:, cols].unsqueeze(2).to_broadcast([P, ND * PAIR // 2, M]),
                                            ALU.mult).then_inc(probs_ready, 1)

            pool.wait_ge(consts_ready, 5)
            rstd1_step(0)
            up_low(0)
            normalise(0)
            rstd2_step(0)
            with pool.Fori(0, NF // 2) as i:
                for slot in range(2):
                    k = i * 2 + slot
                    pool.wait_ge(s_w2[slot], i * 16 + 16)
                    nc.gpsimd.tensor_copy(at_tile(w2_hi, k), w2_stage[:, slot, :]).then_inc(w2_hi_ready, 1)
                    pool.wait_ge(w2_hi_ready, k + 1)
                    nc.gpsimd.tensor_tensor(at_tile(w2_lo, k), w2_stage[:, slot, :], at_tile(w2_hi, k).bitcast(f32),
                                            ALU.subtract).then_inc(w2_lo_ready, 1)
            with pool.Fori(1, TILES) as t:
                rstd1_step(t)
                up_low(t)
                normalise(t)
                rstd2_step(t)

        @block.scalar
        def _(act):
            act.dma_start(c2_raw[:], c2_rows).then_inc(s_c, 16)
            for r in range(REP):
                act.dma_start(c1_rep[r * R:(r + 1) * R, :], c1_w).then_inc(s_c, 16)
            act.dma_start(gates[:, 0:1], g_xattn.unsqueeze(0).to_broadcast([P, 1])).then_inc(s_c, 16)
            act.dma_start(gates[:, 1:2], g_ffn.unsqueeze(0).to_broadcast([P, 1])).then_inc(s_c, 16)

            act.wait_ge(s_c, 16 * (3 + REP))
            nc.scalar.activation(tanh_g[:], gates[:], ACT.Tanh).then_inc(tanh_ready, 1)

            def up_high(t):
                act.wait_ge(up_ready, t + 1)
                wait_past(act, xattn_done, t)
                nc.scalar.activation(up_hi[:], up[:], ACT.Copy).then_inc(up_hi_ready, 1)

            def ctx_high(t):
                wait_past(act, AV_done, t)
                for b in range(PAIR):
                    rs, cs = slice(b * C, (b + 1) * C), slice(b * M, (b + 1) * M)
                    last = nc.scalar.activation(ctx_hi[rs, cs], at_tile(ctx_all, t)[rs, :], ACT.Copy)
                last.then_inc(ctx_hi_ready, 1)

            def AV_high(t):
                act.wait_ge(AV_done, t + 1)
                nc.scalar.activation(flat(AV_hi), att_ps[0][:], ACT.Copy).then_inc(AV_hi_ready, 1)

            def exps(t):
                for half in range(2):
                    act.wait_ge(neg_max_ready, t * 2 + half + 1)
                    for jj in range(ND // 2):
                        for b in range(PAIR):
                            j = half * ND // 2 + jj
                            col = j * PAIR + b
                            at = (jj * PAIR + b) * M
                            last = nc.scalar.activation(probs[:, j, b, :], att_ps[half][:, at:at + M], ACT.Exp,
                                                        bias=neg_max[:, col:col + 1],
                                                        accum_out=row_sum[:, col:col + 1])
                    last.then_inc(exp_ready, 1)

            def PT_high(t):
                for b in range(PAIR):
                    act.wait_ge(probs_turned, t * 2 + b + 1)
                    nc.scalar.activation(PT_hi[:, b, :], att_ps[b][:], ACT.Copy).then_inc(PT_hi_ready, 1)

            def xfT_high(t):
                act.wait_ge(xf_turned, t + 1)
                nc.scalar.activation(flat(xfT_hi), H_ps[0][:], ACT.Copy).then_inc(xfT_hi_ready, 1)

            def t_high(t):
                act.wait_ge(t_done, t + 1)
                nc.scalar.activation(t_parts[0:C, :], inter_ps[0][0:C, 0:P], ACT.Copy).then_inc(t_hi_ready, 1)

            def hT_high(t, g):
                w = GROUPS[g][1] * P
                act.wait_ge(h_turned, t * NG + g + 1)
                nc.scalar.activation(hT_hi[:, g % 2, 0:w], turn_ps[:, 0:w], ACT.Relu).then_inc(hT_hi_ready, 1)

            act.wait_ge(wprod_ready, 1)
            nc.scalar.activation(G_hi[:], H_ps[0][:, 0:P], ACT.Copy, scale=float(C) ** -0.5).then_inc(whi_ready, 1)
            act.wait_ge(wprod_ready, 2)
            nc.scalar.activation(flat(WT_hi), H_ps[1][:, 0:2 * P], ACT.Copy).then_inc(whi_ready, 1)
            act.wait_ge(c1_turned, 1)
            nc.scalar.activation(c1T_hi[:], turn_ps[:], ACT.Copy).then_inc(c1_hi_ready, 1)
            act.wait_ge(s_ctx, 16)
            act.wait_ge(consts_ready, 5)
            ctx_high(0)
            up_high(0)
            AV_high(0)
            exps(0)
            for g, (k0, n) in enumerate(GROUPS):
                act.wait_ge(c2_turned, g + 1)
                nc.scalar.activation(c2T[:, k0 * P:(k0 + n) * P], inter_ps[g % 2][:, 0:n * P], ACT.Copy).then_inc(c2_ready, 1)
            PT_high(0)
            xfT_high(0)
            t_high(0)
            with act.Fori(0, NF // 2) as i:
                for slot in range(2):
                    k = i * 2 + slot
                    act.wait_ge(w1_turned, k + 1)
                    nc.scalar.activation(w1T_hi[:, :, bass.ds(k * P, P)], chunks(H_ps[slot]), ACT.Copy).then_inc(w1_hi_ready, 1)
            with act.Fori(0, TILES - 1) as t:
                ctx_high(t + 1)
                up_high(t + 1)
                AV_high(t + 1)
                hT_high(t, 0)
                exps(t + 1)
                hT_high(t, 1)
                PT_high(t + 1)
                hT_high(t, 2)
                xfT_high(t + 1)
                hT_high(t, 3)
                t_high(t + 1)
            for g in range(NG):
                hT_high(TILES - 1, g)

        @block.vector
        def _(dve):
            nc.vector.memset(doubling[:], 2.0).then_inc(consts2_ready, 1)
            dve.wait_ge(consts2_ready, 1)
            nc.vector.memset(doubling[:].rearrange("p (b i) -> p b i", i=BLK)[:, :, 0:1], 0.0).then_inc(consts2_ready, 1)

            nc.vector.memset(t_parts[C:P, :].bitcast(f32), 0.0).then_inc(consts2_ready, 1)

            def norm1(t):
                one_more = t + 1 if isinstance(t, int) else nc.vector.to_reg(t + 1)
                nc.vector.bn_stats(stats1[:], at_tile(rows, t)).then_inc(stats1_ready, 1)
                dve.wait_ge(consts2_ready, 3)
                dve.wait_ge(stats1_ready, one_more)
                nc.vector.bn_aggr(mv1[:], stats1[:]).then_inc(mv1_ready, 1)

            def up_step(t):
                dve.wait_ge(rstd1_ready, t + 1)
                wait_past(dve, up_lo_ready, t)
                nc.vector.tensor_scalar(up[:], at_tile(rows, t), mv1[:, 0:1], rstd1[:], ALU.subtract, ALU.mult).then_inc(up_ready, 1)

            def ctx_low(t):
                dve.wait_ge(ctx_hi_ready, t + 1)
                wait_past(dve, AV_done, t)
                for b in range(PAIR):
                    rs, cs = slice(b * C, (b + 1) * C), slice(b * M, (b + 1) * M)
                    last = nc.vector.tensor_tensor(ctx_lo[rs, cs], at_tile(ctx_all, t)[rs, :], ctx_hi[rs, cs].bitcast(f32),
                                                   ALU.subtract)
                last.then_inc(ctx_lo_ready, 1)

            def AV_low(t):
                dve.wait_ge(AV_hi_ready, t + 1)
                nc.vector.tensor_tensor(flat(AV_lo), att_ps[0][:], flat(AV_hi).bitcast(f32), ALU.subtract).then_inc(AV_lo_ready, 1)

            def row_max(t):
                dve.wait_ge(energy_done, t + 1)
                for half in range(2):
                    w = ND * PAIR // 2
                    nc.vector.tensor_reduce(neg_max[:, half * w:(half + 1) * w],
                                            att_ps[half][:].rearrange("p (k m) -> p k m", m=M), AX.X, ALU.max,
                                            negate=True).then_inc(neg_max_ready, 1)

            def inv_sums(t):
                for half in range(2):
                    w = ND * PAIR // 2
                    dve.wait_ge(exp_ready, t * 2 + half + 1)
                    nc.vector.reciprocal(inv_sum[:, half * w:(half + 1) * w], row_sum[:, half * w:(half + 1) * w]
                                         ).then_inc(inv_sum_ready, 1)

            def PT_low(t):
                for b in range(PAIR):
                    dve.wait_ge(PT_hi_ready, t * 2 + b + 1)
                    nc.vector.tensor_tensor(PT_lo[:, b, :], att_ps[b][:], PT_hi[:, b, :].bitcast(f32), ALU.subtract
                                            ).then_inc(PT_lo_ready, 1)

            def x2_step(t):
                dve.wait_ge(xattn_done, t + 1)
                nc.vector.scalar_tensor_tensor(at_tile(rows, t), att_ps[0][:], tanh_g[:, 0:1], at_tile(rows, t),
                                               ALU.mult, ALU.add).then_inc(x2_ready, 1)
                dve.wait_ge(consts2_ready, 3)
                dve.wait_ge(x2_ready, t + 1)
                nc.vector.bn_stats(stats2[:], at_tile(rows, t)).then_inc(stats2_ready, 1)
                dve.wait_ge(consts2_ready, 3)
                dve.wait_ge(stats2_ready, t + 1)
                nc.vector.bn_aggr(mv2[:], stats2[:]).then_inc(mv2_ready, 1)

            def xf_step(t):
                dve.wait_ge(rstd2_ready, t + 1)
                nc.vector.tensor_scalar(xf[:], at_tile(rows, t), mv2[:, 0:1], rstd2[:], ALU.subtract, ALU.mult).then_inc(xf_ready, 1)

            def xfT_low(t):
                dve.wait_ge(xfT_hi_ready, t + 1)
                nc.vector.tensor_tensor(flat(xfT_lo), H_ps[0][:], flat(xfT_hi).bitcast(f32), ALU.subtract).then_inc(xfT_lo_ready, 1)

            def t_low(t):
                dve.wait_ge(t_hi_ready, t + 1)
                rs = slice(C // 2, C)
                nc.vector.tensor_tensor(t_parts[rs, :], inter_ps[0][rs, 0:P], t_parts[rs, :].bitcast(f32), ALU.subtract
                                        ).then_inc(t_ready, 1)

            def choose(t, g):
                w = GROUPS[g][1] * P
                n = t * NG + g
                dve.wait_ge(inter_done, n + 1)
                blocks = inter_ps[g % 2][:, 0:w].rearrange("p (b i) -> p b i", i=BLK)
                nc.vector.tensor_reduce(blk_max[:, 0:w // BLK], blocks, AX.X, ALU.max).then_inc(blk_max_ready, 1)
                dve.wait_ge(blk_max_ready, n + 1)
                nc.vector.tensor_tensor(is_max[:, 0:w].rearrange("p (b i) -> p b i", i=BLK), blocks,
                                        blk_max[:, 0:w // BLK].unsqueeze(2).to_broadcast([P, w // BLK, BLK]),
                                        ALU.is_equal).then_inc(is_max_ready, 1)
                dve.wait_ge(is_max_ready, n + 1)
                nc.vector.tensor_tensor_scan(first[:, g % 2, 0:w], doubling[:, 0:w], is_max[:, 0:w], 0.0,
                                             ALU.mult, ALU.add).then_inc(first_ready, 1)

            def mask(t, g):
                w = GROUPS[g][1] * P
                n = t * NG + g
                dve.wait_ge(H_done, n + 1)
                dve.wait_ge(first_ready, n + 1)
                nc.vector.scalar_tensor_tensor(h[:, g % 2, 0:w], first[:, g % 2, 0:w], 1.0, H_ps[g % 2][:, 0:w],
                                               ALU.is_equal, ALU.mult).then_inc(h_ready, 1)

            def hT_low(t, g):
                w = GROUPS[g][1] * P
                dve.wait_ge(hT_hi_ready, t * NG + g + 1)
                nc.vector.scalar_tensor_tensor(hT_lo[:, g % 2, 0:w], turn_ps[:, 0:w], 0.0, hT_hi[:, g % 2, 0:w].bitcast(f32),
                                               ALU.max, ALU.subtract).then_inc(hT_lo_ready, 1)

            def result(t):
                dve.wait_ge(ffn_done, t + 1)
                nc.vector.scalar_tensor_tensor(at_tile(rows, t), ffn_ps[:], tanh_g[:, 1:2], at_tile(rows, t),
                                               ALU.mult, ALU.add).then_inc(out_ready, 1)

            dve.wait_ge(s_x[0], 16)
            norm1(0)
            up_step(0)
            dve.wait_ge(consts_ready, 5)
            ctx_low(0)
            dve.wait_ge(s_c, 16 * (3 + REP))
            nc.vector.tensor_copy(c2_top[:], c2_raw[:]).then_inc(c2_top_ready, 1)
            dve.wait_ge(c2_top_ready, 1)
            for part in range(4):
                if part % 2 == 0:
                    nc.vector.tensor_copy(c2_parts[:, 0:NF, part, :], c2_top[:].bitcast(f32)).then_inc(c2_parts_ready, 1)
                else:
                    nc.vector.tensor_tensor(c2_parts[:, 0:NF, part, :], c2_raw[:], c2_top[:].bitcast(f32), ALU.subtract
                                            ).then_inc(c2_parts_ready, 1)
            dve.wait_ge(whi_ready, 1)
            nc.vector.scalar_tensor_tensor(G_lo[:], H_ps[0][:, 0:P], float(C) ** -0.5, G_hi[:].bitcast(f32),
                                           ALU.mult, ALU.subtract).then_inc(wlo_ready, 1)
            dve.wait_ge(whi_ready, 2)
            nc.vector.tensor_tensor(flat(WT_lo), H_ps[1][:, 0:2 * P], flat(WT_hi).bitcast(f32), ALU.subtract).then_inc(wlo_ready, 1)
            dve.wait_ge(c1_hi_ready, 1)
            nc.vector.tensor_tensor(c1T_lo[:], turn_ps[:], c1T_hi[:].bitcast(f32), ALU.subtract).then_inc(c1_lo_ready, 1)
            AV_low(0)
            row_max(0)
            inv_sums(0)
            PT_low(0)
            dve.wait_ge(tanh_ready, 1)
            x2_step(0)
            xf_step(0)
            xfT_low(0)
            t_low(0)
            with dve.Fori(0, NF // 2) as i:
                for slot in range(2):
                    k = i * 2 + slot
                    dve.wait_ge(w1_hi_ready, k + 1)
                    nc.vector.tensor_tensor(w1T_lo[:, :, bass.ds(k * P, P)], chunks(H_ps[slot]),
                                            w1T_hi[:, :, bass.ds(k * P, P)].bitcast(f32), ALU.subtract).then_inc(w1_lo_ready, 1)
            dve.wait_ge(s_x[1], 16)
            with dve.Fori(0, TILES - 1) as t:
                norm1(t + 1)
                ctx_low(t + 1)
                choose(t, 0)
                up_step(t + 1)
                choose(t, 1)
                AV_low(t + 1)
                mask(t, 0)
                mask(t, 1)
                row_max(t + 1)
                hT_low(t, 0)
                choose(t, 2)
                inv_sums(t + 1)
                mask(t, 2)
                hT_low(t, 1)
                PT_low(t + 1)
                choose(t, 3)
                x2_step(t + 1)
                mask(t, 3)
                hT_low(t, 2)
                xf_step(t + 1)
                xfT_low(t + 1)
                hT_low(t, 3)
                t_low(t + 1)
                result(t)
            t = TILES - 1
            choose(t, 0)
            choose(t, 1)
            for g in range(NG):
                mask(t, g)
                hT_low(t, g)
                if g + 2 < NG:
                    choose(t, g + 2)
            result(t)

        @block.tensor
        def _(pe):
            def AV(t):
                pe.wait_ge(ctx_lo_ready, t + 1)
                wait_past(pe, x2_ready, t)
                three_passes(att_ps[0][:, 0:PAIR * M], G_hi[:], G_lo[:], ctx_hi[:], ctx_lo[:])
                for b in range(PAIR):
                    ms = slice(b * M, (b + 1) * M)
                    cs = slice((PAIR + b) * P, (PAIR + b + 1) * P)
                    last = three_passes(att_ps[0][:, cs], ctx_hi[:, ms], ctx_lo[:, ms], WT_hi[:, 0, :], WT_lo[:, 0, :])
                last.then_inc(AV_done, 1)

            def energy(t):
                pe.wait_ge(AV_lo_ready, t + 1)
                pe.wait_ge(up_lo_ready, t + 1)
                for j in range(ND):
                    js = slice(j * P, (j + 1) * P)
                    cs = slice(j % 2 * PAIR * M, (j % 2 + 1) * PAIR * M)
                    last = three_passes(att_ps[j // 2][:, cs], up_hi[:, js], up_lo[:, js], AV_hi[:, 0:PAIR, :], AV_lo[:, 0:PAIR, :])
                last.then_inc(energy_done, 1)

            def turn_probs(t):
                pe.wait_ge(probs_ready, t * 2 + 2)
                for b in range(PAIR):
                    for j in range(ND):
                        last = nc.tensor.transpose(att_ps[b][:, j * P:(j + 1) * P], probs[:, j, b, :], ident[:])
                    last.then_inc(probs_turned, 1)

            def xattn(t):
                pe.wait_ge(PT_lo_ready, t * 2 + 1)
                three_passes(att_ps[0][:], WT_hi[:, 1, :], WT_lo[:, 1, :], up_hi[:], up_lo[:], True, False)
                for b in range(PAIR):
                    pe.wait_ge(PT_lo_ready, t * 2 + b + 1)
                    last = three_passes(att_ps[0][:], AV_hi[:, PAIR + b, :], AV_lo[:, PAIR + b, :], PT_hi[:, b, :], PT_lo[:, b, :],
                                        False, b == PAIR - 1)
                last.then_inc(xattn_done, 1)

            def turn_xf(t):
                pe.wait_ge(xf_ready, t + 1)
                for d in range(ND):
                    last = nc.tensor.transpose(H_ps[0][:, d * P:(d + 1) * P], xf[:, d * P:(d + 1) * P], ident[:])
                last.then_inc(xf_turned, 1)

            def low_rank(t):
                pe.wait_ge(xfT_lo_ready, t + 1)
                for d in range(ND):
                    ds = slice(d * P, (d + 1) * P)
                    last = three_passes(inter_ps[0][:, 0:P], c1T_hi[:, ds], c1T_lo[:, ds], xfT_hi[:, d, :], xfT_lo[:, d, :],
                                        d == 0, d == ND - 1)
                last.then_inc(t_done, 1)

            def inter(t, g):
                k0, n = GROUPS[g]
                if g == 0:
                    pe.wait_ge(t_ready, t + 1)
                if g >= 2:
                    pe.wait_ge(is_max_ready, t * NG + g - 1)
                nc.tensor.matmul(inter_ps[g % 2][:, 0:n * P], t_parts[:], c2T[:, k0 * P:(k0 + n) * P],
                                 start=True, stop=True).then_inc(inter_done, 1)

            def H(t, g):
                k0, n = GROUPS[g]
                fs = slice(k0 * P, (k0 + n) * P)
                if g >= 2:
                    pe.wait_ge(h_ready, t * NG + g - 1)
                for d in range(ND):
                    last = three_passes(H_ps[g % 2][:, 0:n * P], xfT_hi[:, d, :], xfT_lo[:, d, :], w1T_hi[:, d, fs], w1T_lo[:, d, fs],
                                        d == 0, d == ND - 1)
                last.then_inc(H_done, 1)

            def turn_h(t, g):
                pe.wait_ge(h_ready, t * NG + g + 1)
                if g >= 1:
                    pe.wait_ge(hT_lo_ready, t * NG + g)
                for k in range(GROUPS[g][1]):
                    ks = slice(k * P, (k + 1) * P)
                    last = nc.tensor.transpose(turn_ps[:, ks], h[:, g % 2, ks], ident[:])
                last.then_inc(h_turned, 1)

            def down(t, g):
                k0, n = GROUPS[g]
                pe.wait_ge(hT_lo_ready, t * NG + g + 1)
                pe.wait_ge(w2_lo_ready, k0 + n)
                for k in range(n):
                    ks = slice(k * P, (k + 1) * P)
                    last = three_passes(ffn_ps[:], hT_hi[:, g % 2, ks], hT_lo[:, g % 2, ks], w2_hi[:, k0 + k, :], w2_lo[:, k0 + k, :],
                                        k0 + k == 0, k0 + k == NF - 1)
                if g == NG - 1:
                    last.then_inc(ffn_done, 1)

            pe.wait_ge(ident_ready, 1)
            pe.wait_ge(consts2_ready, 3)
            pe.wait_ge(s_small, 16 * 4 * PAIR)
            nc.tensor.matmul(H_ps[0][:, 0:P], W_bd[:, 0, :], W_bd[:, 1, :], start=True, stop=True).then_inc(wprod_ready, 1)
            for n in range(2):
                last = nc.tensor.transpose(H_ps[1][:, n * P:(n + 1) * P], W_bd[:, 2 + n, :], ident[:])
            last.then_inc(wprod_ready, 1)
            pe.wait_ge(s_c, 16 * (3 + REP))
            for d in range(ND):
                last = nc.tensor.transpose(turn_ps[:, d * P:(d + 1) * P], c1_rep[:, d * P:(d + 1) * P], ident[:])
            last.then_inc(c1_turned, 1)
            pe.wait_ge(wlo_ready, 2)
            AV(0)
            energy(0)
            pe.wait_ge(c2_parts_ready, 4)
            pe.wait_ge(consts_ready, 5)
            for g, (k0, n) in enumerate(GROUPS):
                if g >= 2:
                    pe.wait_ge(c2_ready, g - 1)
                for k in range(n):
                    last = nc.tensor.transpose(inter_ps[g % 2][:, k * P:(k + 1) * P],
                                               c2_parts[:, k0 + k:k0 + k + 2, :, :].rearrange("p k a r -> p (k a r)"), ident[:])
                last.then_inc(c2_turned, 1)
            turn_probs(0)
            xattn(0)
            turn_xf(0)
            pe.wait_ge(c1_lo_ready, 1)
            pe.wait_ge(c2_ready, NG)
            low_rank(0)
            for k in range(2):
                pe.wait_ge(s_w1[k], 16)
                for d in range(ND):
                    last = nc.tensor.transpose(H_ps[k][:, d * P:(d + 1) * P], w1_stage[:, k, d * P:(d + 1) * P], ident[:])
                last.then_inc(w1_turned, 1)
            with pe.Fori(1, NF // 2) as i:
                for slot in range(2):
                    pe.wait_ge(s_w1[slot], i * 16 + 16)
                    pe.wait_ge(w1_lo_ready, i * 2 + slot - 1)
                    for d in range(ND):
                        last = nc.tensor.transpose(H_ps[slot][:, d * P:(d + 1) * P], w1_stage[:, slot, d * P:(d + 1) * P], ident[:])
                    last.then_inc(w1_turned, 1)
            pe.wait_ge(w1_lo_ready, NF)
            with pe.Fori(0, TILES - 1) as t:
                inter(t, 0)
                inter(t, 1)
                AV(t + 1)
                H(t, 0)
                H(t, 1)
                energy(t + 1)
                turn_h(t, 0)
                inter(t, 2)
                H(t, 2)
                down(t, 0)
                turn_h(t, 1)
                turn_probs(t + 1)
                inter(t, 3)
                H(t, 3)
                xattn(t + 1)
                down(t, 1)
                turn_h(t, 2)
                down(t, 2)
                turn_xf(t + 1)
                turn_h(t, 3)
                low_rank(t + 1)
                down(t, 3)
            t = TILES - 1
            inter(t, 0)
            inter(t, 1)
            H(t, 0)
            H(t, 1)
            for g in range(NG):
                turn_h(t, g)
                if g + 2 < NG:
                    inter(t, g + 2)
                    H(t, g + 2)
                down(t, g)


_INS = ['x', 'ctx_1024', 'g_xattn', 'g_ffn', 'L0_xattn_Wq', 'L0_xattn_Wk', 'L0_xattn_Wv', 'L0_xattn_Wskip',
        'L0_ffn_c1_w', 'L0_ffn_c2_w', 'L0_ffn_w1', 'L0_ffn_w2t']


def kernel(**inputs):
    import numpy as np
    import concourse.bacc as bacc
    from concourse.bass_utils import run_bass_kernel_spmd

    nc = bacc.Bacc("TRN2", target_bir_lowering=False, num_devices=1)
    arrays, args = {}, []
    for name in _INS:
        a = np.ascontiguousarray(inputs[name])
        arrays[f"in_{name}"] = a
        args.append(nc.dram_tensor(f"in_{name}", a.shape, mybir.dt.from_np(a.dtype), kind="ExternalInput").ap())
    x = arrays["in_x"]
    args.append(nc.dram_tensor("out", x.shape, mybir.dt.from_np(x.dtype), kind="ExternalOutput").ap())
    flamingo_gated_layer(nc, *args)
    r = run_bass_kernel_spmd(nc, [arrays], core_ids=[0])
    return r.results[0]["out"]
```

```python
import concourse.bass as bass
from concourse import mybir
from contextlib import ExitStack


def flamingo_gated_layer(
    nc: bass.Bass,
    x: bass.AP,
    ctx: bass.AP,
    g_xattn: bass.AP,
    g_ffn: bass.AP,
    Wq: bass.AP,
    Wk: bass.AP,
    Wv: bass.AP,
    Wskip: bass.AP,
    c1_w: bass.AP,
    c2_w: bass.AP,
    w1: bass.AP,
    w2t: bass.AP,
    out: bass.AP,
):
    f32 = mybir.dt.float32
    f32r = mybir.dt.float32r
    bf16 = mybir.dt.bfloat16
    ALU = mybir.AluOpType
    ACT = mybir.ActivationFunctionType
    AX = mybir.AxisListType

    P = 128
    B, C, N = x.shape
    M = ctx.shape[2]
    R = c1_w.shape[0]
    F = w1.shape[0]
    BLK = 32
    TILES = B * C // P
    PAIR = P // C
    ND = N // P
    NF = F // P
    GF = 4
    GROUPS = [(g, min(GF, NF - g)) for g in range(0, NF, GF)]
    NG = len(GROUPS)
    GW = GF * P
    EPS = 1e-5
    REP = P // R
    W1_SLOTS = TILES - 1
    W2_SLOTS = 4

    x_rows = x.rearrange("(t b) c n -> (b c) t n", b=PAIR)
    out_rows = out.rearrange("(t b) c n -> (b c) t n", b=PAIR)
    ctx_rows = ctx.rearrange("(t b) c m -> (b c) t m", b=PAIR)
    w1_rows = w1.rearrange("(k p) n -> p k n", p=P)
    w2_rows = w2t.rearrange("(k p) n -> p k n", p=P)
    c2_rows = c2_w.rearrange("(k p) r -> p k r", p=P)

    stack = ExitStack()
    with stack:
        def sb(name, shape, dt=f32):
            return stack.enter_context(nc.sbuf_tensor(name, shape, dt))

        def bank(name):
            return stack.enter_context(nc.psum_tensor(name, [P, 512], f32))

        def sem(name):
            return stack.enter_context(nc.semaphore(name))

        w1T_hi = sb("w1T_hi", [P, ND, F], f32r)
        w1T_lo = sb("w1T_lo", [P, ND, F], f32r)
        w2_hi = sb("w2_hi", [P, NF, N], f32r)
        w2_lo = sb("w2_lo", [P, NF, N], f32r)
        c2T = sb("c2T", [P, F], f32r)
        c1T_parts = sb("c1T_parts", [P, ND, 2, P // 2], f32r)
        G_hi = sb("G_hi", [P, P], f32r)
        G_lo = sb("G_lo", [P, P], f32r)
        WT_hi = sb("WT_hi", [P, 2, P], f32r)
        WT_lo = sb("WT_lo", [P, 2, P], f32r)
        ident = sb("ident", [P, P])
        doubling = sb("doubling", [P, GW], bf16)
        minus_half = sb("minus_half", [P, 1])
        eps = sb("eps", [P, 1])
        over_n = sb("over_n", [P, 1])
        minus_over_n = sb("minus_over_n", [P, 1])
        gates = sb("gates", [P, 2])
        tanh_g = sb("tanh_g", [P, 2])
        W_in = sb("W_in", [P, 4, C])
        W_bd = sb("W_bd", [P, 4, P])
        c2_raw = sb("c2_raw", [P, NF, R])
        w2_stage = sb("w2_stage", [P, W2_SLOTS, N])
        rows = sb("rows", [P, TILES, N])
        x_sum = sb("x_sum", [P, 1])
        neg_mean = sb("neg_mean", [P, 1])
        square_sum = sb("square_sum", [P, 1])
        var_eps = sb("var_eps", [P, 1])
        rstd1 = sb("rstd1", [P, 1])
        centred = sb("centred", [P, N])
        up = sb("up", [P, N])
        up_hi = sb("up_hi", [P, N], f32r)
        up_lo = sb("up_lo", [P, N], f32r)
        ctx_all = sb("ctx_all", [P, TILES, M])
        ctx_hi = sb("ctx_hi", [P, M], f32r)
        ctx_lo = sb("ctx_lo", [P, M], f32r)
        A_hi = sb("A_hi", [P, PAIR * M], f32r)
        A_lo = sb("A_lo", [P, PAIR * M], f32r)
        v_hi = sb("v_hi", [P, 2 * PAIR, C], f32r)
        v_lo = sb("v_lo", [P, 2 * PAIR, C], f32r)
        neg_max = sb("neg_max", [P, ND * PAIR])
        row_sum = sb("row_sum", [P, ND * PAIR])
        inv_sum = sb("inv_sum", [P, ND * PAIR])
        probs = sb("probs", [P, ND, PAIR, M])
        PT_hi = sb("PT_hi", [P, PAIR, N], f32r)
        PT_lo = sb("PT_lo", [P, PAIR, N], f32r)
        stats2 = sb("stats2", [P, 6])
        mv2 = sb("mv2", [P, 2])
        rstd2 = sb("rstd2", [P, 1])
        xf = sb("xf", [P, N])
        xfT_hi = sb("xfT_hi", [P, ND, P], f32r)
        xfT_lo = sb("xfT_lo", [P, ND, P], f32r)
        t_parts = sb("t_parts", [P, P], f32r)
        blk_max = sb("blk_max", [P, GW // BLK])
        is_max = sb("is_max", [P, GW], bf16)
        first = sb("first", [P, 2, GW], bf16)
        h = sb("h", [P, 2, GW])
        hT_hi = sb("hT_hi", [P, 2, GW], f32r)
        hT_lo = sb("hT_lo", [P, 2, GW], f32r)
        c1_rep = xf
        c2_parts = h[:].rearrange("p a b -> p (a b)")[:, 0:(NF + 1) * 4 * R].rearrange("p (k a r) -> p k a r", a=4, r=R)

        inter_ps = [bank("inter0"), bank("inter1")]
        H_ps = [bank("H0"), bank("H1")]
        turn_ps = bank("turn")
        ffn_ps = bank("ffn")
        att_ps = [bank("att0"), bank("att1")]

        s_x = [sem("x0_in"), sem("xrest_in")]
        s_small = sem("small_in")
        s_c1 = sem("c1_in")
        s_c2 = sem("c2_in")
        s_g = sem("gates_in")
        s_ctx = sem("ctx_in")
        s_w1 = [sem(f"w1_slot{n}_in") for n in range(W1_SLOTS)]
        s_w2 = [sem(f"w2_slot{n}_in") for n in range(W2_SLOTS)]
        s_out = sem("out_written")
        zeroed = sem("zeroed")
        ident_ready = sem("ident_ready")
        consts_ready = sem("consts_ready")
        tanh_ready = sem("tanh_ready")
        wprod_ready = sem("wprod_ready")
        whi_ready = sem("whi_ready")
        wlo_ready = sem("wlo_ready")
        w1_turned = sem("w1_turned")
        w1_hi_ready = sem("w1_hi_ready")
        w1_lo_ready = sem("w1_lo_ready")
        W_bd_ready = sem("W_bd_ready")
        w2_hi_ready = sem("w2_hi_ready")
        w2_lo_even_ready = sem("w2_lo_even_ready")
        w2_lo_odd_ready = sem("w2_lo_odd_ready")
        c1_turned = sem("c1_turned")
        c1_hi_ready = sem("c1_hi_ready")
        c1_lo_ready = sem("c1_lo_ready")
        c2_top_ready = sem("c2_top_ready")
        c2_parts_ready = sem("c2_parts_ready")
        c2_turned = sem("c2_turned")
        c2_ready = sem("c2_ready")
        consts2_ready = sem("consts2_ready")

        x_sum_ready = sem("x_sum_ready")
        neg_mean_ready = sem("neg_mean_ready")
        centred_ready = sem("centred_ready")
        square_sum_ready = sem("square_sum_ready")
        rstd1_ready = sem("rstd1_ready")
        up_ready = sem("up_ready")
        up_hi_ready = sem("up_hi_ready")
        up_lo_ready = sem("up_lo_ready")
        ctx_hi_ready = sem("ctx_hi_ready")
        ctx_lo_ready = sem("ctx_lo_ready")
        AV_done = sem("AV_done")
        AV_hi_ready = sem("AV_hi_ready")
        AV_lo_ready = sem("AV_lo_ready")
        energy_done = sem("energy_done")
        neg_max_ready = sem("neg_max_ready")
        exp_ready = sem("exp_ready")
        inv_sum_ready = sem("inv_sum_ready")
        probs_ready = sem("probs_ready")
        probs_turned = sem("probs_turned")
        PT_hi_ready = sem("PT_hi_ready")
        PT_lo_ready = sem("PT_lo_ready")
        xattn_done = sem("xattn_done")
        x2_ready = sem("x2_ready")
        stats2_ready = sem("stats2_ready")
        mv2_ready = sem("mv2_ready")
        var1_ready = sem("var1_ready")
        var2_ready = sem("var2_ready")
        rstd2_ready = sem("rstd2_ready")
        xf_ready = sem("xf_ready")
        xf_turned = sem("xf_turned")
        xfT_hi_ready = sem("xfT_hi_ready")
        xfT_lo_ready = sem("xfT_lo_ready")
        t_done = sem("t_done")
        t_hi_ready = sem("t_hi_ready")
        t_ready = sem("t_ready")
        inter_done = sem("inter_done")
        blk_max_ready = sem("blk_max_ready")
        is_max_ready = sem("is_max_ready")
        first_ready = sem("first_ready")
        H_done = sem("H_done")
        h_ready = sem("h_ready")
        h_turned = sem("h_turned")
        hT_hi_ready = sem("hT_hi_ready")
        hT_lo_ready = sem("hT_lo_ready")
        ffn_done = sem("ffn_done")
        out_ready = sem("out_ready")

        def wait_past(eng, semaphore, n):
            if not isinstance(n, int) or n > 0:
                eng.wait_ge(semaphore, n)

        CONSTS = 9

        def flat(buf):
            return buf[:].rearrange("p a b -> p (a b)")

        def flat2(ap):
            return ap.rearrange("p a b -> p (a b)")

        def chunks(ps):
            return ps[:].rearrange("p (d f) -> p d f", d=ND)

        def at_tile(buf, t):
            return buf[:, bass.ds(t, 1), :].rearrange("p o w -> p (o w)")

        def three_passes(ps, lhs_hi, lhs_lo, rhs_hi, rhs_lo, start=True, stop=True):
            nc.tensor.matmul(ps, lhs_hi, rhs_hi, start=start, stop=False)
            nc.tensor.matmul(ps, lhs_hi, rhs_lo, start=False, stop=False)
            return nc.tensor.matmul(ps, lhs_lo, rhs_hi, start=False, stop=stop)

        block = stack.enter_context(nc.Block())

        @block.sync
        def _(sp):
            sp.dma_start(rows[:, 0, :], x_rows[:, 0, :]).then_inc(s_x[0], 16)
            for n, w in enumerate((Wk, Wq, Wv, Wskip)):
                for b in range(PAIR):
                    sp.dma_start(W_in[b * C:(b + 1) * C, n, :], w).then_inc(s_small, 16)
            sp.dma_start(ctx_all[:], ctx_rows).then_inc(s_ctx, 16)
            for k in range(NF):
                slot = k % W1_SLOTS
                if k >= W1_SLOTS:
                    sp.wait_ge(w1_turned, k - W1_SLOTS + 1)
                sp.dma_start(rows[:, 1 + slot, :], w1_rows[:, k, :]).then_inc(s_w1[slot], 16)
            for k in range(NF):
                slot = k % W2_SLOTS
                if k >= W2_SLOTS:
                    sp.wait_ge(w2_lo_odd_ready if k % 2 else w2_lo_even_ready, (k - W2_SLOTS) // 2 + 1)
                sp.dma_start(w2_stage[:, slot, :], w2_rows[:, k, :]).then_inc(s_w2[slot], 16)
                if k == 7:
                    sp.wait_ge(w1_turned, NF)
                    sp.dma_start(rows[:, 1, :], x_rows[:, 1, :]).then_inc(s_x[1], 16)
            sp.dma_start(rows[:, 2:, :], x_rows[:, 2:, :]).then_inc(s_x[1], 16)
            with sp.Fori(0, TILES) as t:
                sp.wait_ge(out_ready, t + 1)
                sp.dma_start(out_rows[:, bass.ds(t, 1), :], rows[:, bass.ds(t, 1), :]).then_inc(s_out, 16)
            sp.wait_ge(s_out, 16 * TILES)

        @block.gpsimd
        def _(pool):
            nc.gpsimd.memset(ident[:], 0.0).then_inc(zeroed, 1)
            nc.gpsimd.memset(minus_half[:], -0.5).then_inc(consts_ready, 1)
            nc.gpsimd.memset(eps[:], EPS).then_inc(consts_ready, 1)
            nc.gpsimd.memset(over_n[:], 1.0 / N).then_inc(consts_ready, 1)
            nc.gpsimd.memset(minus_over_n[:], -1.0 / N).then_inc(consts_ready, 1)
            nc.gpsimd.memset(c2_parts[:, NF, :, :], 0.0).then_inc(consts_ready, 1)
            for buf in (A_hi[:], A_lo[:], v_hi[:], v_lo[:]):
                nc.gpsimd.memset(buf.bitcast(f32), 0.0).then_inc(consts_ready, 1)
            pool.wait_ge(zeroed, 1)
            nc.gpsimd.affine_select(out=ident[:], in_=ident[:], compare_op=ALU.not_equal, fill=1.0, base=0,
                                    pattern=[[-1, P]], channel_multiplier=1).then_inc(ident_ready, 1)

            def mean1(t):
                pool.wait_ge(x_sum_ready, t + 1)
                nc.gpsimd.tensor_tensor(neg_mean[:], x_sum[:], minus_over_n[:], ALU.mult).then_inc(neg_mean_ready, 1)

            def rstd1_step(t):
                pool.wait_ge(square_sum_ready, t + 1)
                nc.gpsimd.tensor_tensor(var_eps[:], square_sum[:], over_n[:], ALU.mult).then_inc(var1_ready, 1)
                pool.wait_ge(var1_ready, t * 2 + 1)
                nc.gpsimd.tensor_tensor(var_eps[:], var_eps[:], eps[:], ALU.add).then_inc(var1_ready, 1)
                pool.wait_ge(var1_ready, t * 2 + 2)
                nc.gpsimd.tensor_tensor(rstd1[:], var_eps[:], minus_half[:], ALU.pow).then_inc(rstd1_ready, 1)

            def ctx_low(t):
                pool.wait_ge(ctx_hi_ready, t + 1)
                nc.gpsimd.tensor_tensor(ctx_lo[:], at_tile(ctx_all, t), ctx_hi[:].bitcast(f32), ALU.subtract).then_inc(ctx_lo_ready, 1)

            def rstd2_step(t):
                pool.wait_ge(mv2_ready, t + 1)
                nc.gpsimd.tensor_tensor(rstd2[:], mv2[:, 1:2], eps[:], ALU.add).then_inc(var2_ready, 1)
                pool.wait_ge(var2_ready, t + 1)
                nc.gpsimd.tensor_tensor(rstd2[:], rstd2[:], minus_half[:], ALU.pow).then_inc(rstd2_ready, 1)

            def up_low(t):
                pool.wait_ge(up_hi_ready, t + 1)
                nc.gpsimd.tensor_tensor(up_lo[:], up[:], up_hi[:].bitcast(f32), ALU.subtract).then_inc(up_lo_ready, 1)

            def normalise(t):
                for half in range(2):
                    pool.wait_ge(inv_sum_ready, t * 2 + half + 1)
                    js = slice(half * ND // 2, (half + 1) * ND // 2)
                    cols = slice(half * ND * PAIR // 2, (half + 1) * ND * PAIR // 2)
                    pr = probs[:, js, :, :].rearrange("p j b m -> p (j b) m")
                    nc.gpsimd.tensor_tensor(pr, pr, inv_sum[:, cols].unsqueeze(2).to_broadcast([P, ND * PAIR // 2, M]),
                                            ALU.mult).then_inc(probs_ready, 1)

            def w2_low(k):
                slot = k % W2_SLOTS
                pool.wait_ge(w2_hi_ready, k + 1)
                nc.gpsimd.tensor_tensor(w2_lo[:, k, :], w2_stage[:, slot, :], w2_hi[:, k, :].bitcast(f32),
                                        ALU.subtract).then_inc(w2_lo_even_ready, 1)

            pool.wait_ge(consts_ready, CONSTS)
            mean1(0)
            ctx_low(0)
            rstd1_step(0)
            up_low(0)
            normalise(0)
            for k in (0, 2):
                w2_low(k)
            rstd2_step(0)
            for k in range(4, NF, 2):
                w2_low(k)
            with pool.Fori(1, TILES) as t:
                ctx_low(t)
                mean1(t)
                rstd1_step(t)
                up_low(t)
                normalise(t)
                rstd2_step(t)

        @block.scalar
        def _(act):
            act.dma_start(c2_raw[:], c2_rows).then_inc(s_c2, 16)
            for r in range(REP):
                act.dma_start(c1_rep[r * R:(r + 1) * R, :], c1_w).then_inc(s_c1, 16)
            act.dma_start(gates[:, 0:1], g_xattn.unsqueeze(0).to_broadcast([P, 1])).then_inc(s_g, 16)
            act.dma_start(gates[:, 1:2], g_ffn.unsqueeze(0).to_broadcast([P, 1])).then_inc(s_g, 16)

            def norm1(t):
                nc.scalar.activation(centred[:], at_tile(rows, t), ACT.Copy, accum_out=x_sum[:]).then_inc(x_sum_ready, 1)
                ctx_high(t)
                act.wait_ge(neg_mean_ready, t + 1)
                nc.scalar.activation(centred[:], centred[:], ACT.Identity, bias=neg_mean[:]).then_inc(centred_ready, 1)
                act.wait_ge(centred_ready, t + 1)
                nc.scalar.activation(up[:], centred[:], ACT.Square, accum_out=square_sum[:]).then_inc(square_sum_ready, 1)
                act.wait_ge(rstd1_ready, t + 1)
                nc.scalar.activation(up[:], centred[:], ACT.Copy, scale=rstd1[:]).then_inc(up_ready, 1)
                act.wait_ge(up_ready, t + 1)
                nc.scalar.activation(up_hi[:], up[:], ACT.Copy).then_inc(up_hi_ready, 1)

            def ctx_high(t):
                nc.scalar.activation(ctx_hi[:], at_tile(ctx_all, t), ACT.Copy).then_inc(ctx_hi_ready, 1)

            def AV_high(t):
                act.wait_ge(AV_done, t + 1)
                for b in range(PAIR):
                    rs = slice(b * C, (b + 1) * C)
                    nc.scalar.activation(A_hi[rs, b * M:(b + 1) * M], att_ps[0][rs, 0:M], ACT.Copy)
                nc.scalar.activation(v_hi[:, 0:2 * PAIR:PAIR + 1, :], att_ps[0][:, M:2 * M].rearrange("p (b c) -> p b c", b=PAIR),
                                     ACT.Copy).then_inc(AV_hi_ready, 1)

            def exps(t):
                for half in range(2):
                    act.wait_ge(neg_max_ready, t * 2 + half + 1)
                    for jj in range(ND // 2):
                        for b in range(PAIR):
                            j = half * ND // 2 + jj
                            col = j * PAIR + b
                            at = (jj * PAIR + b) * M
                            last = nc.scalar.activation(probs[:, j, b, :], att_ps[half][:, at:at + M], ACT.Exp,
                                                        bias=neg_max[:, col:col + 1],
                                                        accum_out=row_sum[:, col:col + 1])
                    last.then_inc(exp_ready, 1)

            def PT_high(t):
                for b in range(PAIR):
                    act.wait_ge(probs_turned, t * 2 + b + 1)
                    nc.scalar.activation(PT_hi[:, b, :], att_ps[b][:], ACT.Copy).then_inc(PT_hi_ready, 1)

            def xfT_high(t):
                act.wait_ge(xf_turned, t + 1)
                nc.scalar.activation(flat(xfT_hi), H_ps[0][:], ACT.Copy).then_inc(xfT_hi_ready, 1)

            def t_high(t):
                act.wait_ge(t_done, t + 1)
                nc.scalar.activation(t_parts[:], inter_ps[0][:, 0:P], ACT.Copy).then_inc(t_hi_ready, 1)

            def hT_high(t, g):
                w = GROUPS[g][1] * P
                act.wait_ge(h_turned, t * NG + g + 1)
                nc.scalar.activation(hT_hi[:, g % 2, 0:w], turn_ps[:, 0:w], ACT.Relu).then_inc(hT_hi_ready, 1)

            def w1_high(k0, k1):
                for k in range(k0, k1):
                    act.wait_ge(w1_turned, k + 1)
                    nc.scalar.activation(w1T_hi[:, :, k * P:(k + 1) * P], chunks(H_ps[k % 2]), ACT.Copy).then_inc(w1_hi_ready, 1)

            def w2_high(k0, k1):
                for k in range(k0, k1):
                    slot = k % W2_SLOTS
                    act.wait_ge(s_w2[slot], 16 * (k // W2_SLOTS + 1))
                    nc.scalar.activation(w2_hi[:, k, :], w2_stage[:, slot, :], ACT.Copy).then_inc(w2_hi_ready, 1)

            act.wait_ge(s_x[0], 16)
            act.wait_ge(s_ctx, 16)
            norm1(0)
            act.wait_ge(wprod_ready, 1)
            nc.scalar.activation(G_hi[:], H_ps[0][:, 0:P], ACT.Copy, scale=float(C) ** -0.5).then_inc(whi_ready, 1)
            act.wait_ge(wprod_ready, 2)
            nc.scalar.activation(flat(WT_hi), H_ps[1][:, 0:2 * P], ACT.Copy).then_inc(whi_ready, 1)
            act.wait_ge(consts_ready, CONSTS)
            AV_high(0)
            act.wait_ge(c1_turned, 1)
            nc.scalar.activation(c1T_parts[:, :, 0, :], chunks(turn_ps)[:, :, 0:P // 2], ACT.Copy).then_inc(c1_hi_ready, 1)
            act.wait_ge(s_g, 16 * 2)
            nc.scalar.activation(tanh_g[:], gates[:], ACT.Tanh).then_inc(tanh_ready, 1)
            w1_high(0, 2)
            exps(0)
            w1_high(2, 7)
            for g, (k0, n) in enumerate(GROUPS):
                act.wait_ge(c2_turned, g + 1)
                for half in range(2):
                    last = nc.scalar.activation(c2T[half * C:(half + 1) * C, k0 * P:(k0 + n) * P], inter_ps[g % 2][0:C, 0:n * P],
                                                ACT.Copy)
                last.then_inc(c2_ready, 1)
            PT_high(0)
            w1_high(7, NF)
            w2_high(0, 6)
            xfT_high(0)
            w2_high(6, 10)
            t_high(0)
            w2_high(10, NF)
            act.wait_ge(s_x[1], 32)
            with act.Fori(0, TILES - 1) as t:
                norm1(t + 1)
                AV_high(t + 1)
                hT_high(t, 0)
                hT_high(t, 1)
                exps(t + 1)
                PT_high(t + 1)
                hT_high(t, 2)
                hT_high(t, 3)
                xfT_high(t + 1)
                t_high(t + 1)
            for g in range(NG):
                hT_high(TILES - 1, g)

        @block.vector
        def _(dve):
            nc.vector.memset(doubling[:], 2.0).then_inc(consts2_ready, 1)
            dve.wait_ge(consts2_ready, 1)
            nc.vector.memset(doubling[:].rearrange("p (b i) -> p b i", i=BLK)[:, :, 0:1], 0.0).then_inc(consts2_ready, 1)

            def AV_low(t):
                dve.wait_ge(AV_hi_ready, t + 1)
                for b in range(PAIR):
                    rs, cs = slice(b * C, (b + 1) * C), slice(b * M, (b + 1) * M)
                    nc.vector.tensor_tensor(A_lo[rs, cs], att_ps[0][rs, 0:M], A_hi[rs, cs].bitcast(f32), ALU.subtract)
                nc.vector.tensor_tensor(v_lo[:, 0:2 * PAIR:PAIR + 1, :], att_ps[0][:, M:2 * M].rearrange("p (b c) -> p b c", b=PAIR),
                                        v_hi[:, 0:2 * PAIR:PAIR + 1, :].bitcast(f32), ALU.subtract).then_inc(AV_lo_ready, 1)

            def row_max(t):
                dve.wait_ge(energy_done, t + 1)
                for half in range(2):
                    w = ND * PAIR // 2
                    nc.vector.tensor_reduce(neg_max[:, half * w:(half + 1) * w],
                                            att_ps[half][:].rearrange("p (k m) -> p k m", m=M), AX.X, ALU.max,
                                            negate=True).then_inc(neg_max_ready, 1)

            def inv_sums(t):
                for half in range(2):
                    w = ND * PAIR // 2
                    dve.wait_ge(exp_ready, t * 2 + half + 1)
                    nc.vector.reciprocal(inv_sum[:, half * w:(half + 1) * w], row_sum[:, half * w:(half + 1) * w]
                                         ).then_inc(inv_sum_ready, 1)

            def PT_low(t):
                for b in range(PAIR):
                    dve.wait_ge(PT_hi_ready, t * 2 + b + 1)
                    nc.vector.tensor_tensor(PT_lo[:, b, :], att_ps[b][:], PT_hi[:, b, :].bitcast(f32), ALU.subtract
                                            ).then_inc(PT_lo_ready, 1)

            def x2_step(t):
                dve.wait_ge(xattn_done, t + 1)
                nc.vector.scalar_tensor_tensor(at_tile(rows, t), att_ps[0][:], tanh_g[:, 0:1], at_tile(rows, t),
                                               ALU.mult, ALU.add).then_inc(x2_ready, 1)
                dve.wait_ge(consts2_ready, 2)
                dve.wait_ge(x2_ready, t + 1)
                nc.vector.bn_stats(stats2[:], at_tile(rows, t)).then_inc(stats2_ready, 1)
                dve.wait_ge(consts2_ready, 2)
                dve.wait_ge(stats2_ready, t + 1)
                nc.vector.bn_aggr(mv2[:], stats2[:]).then_inc(mv2_ready, 1)

            def xf_step(t):
                dve.wait_ge(rstd2_ready, t + 1)
                nc.vector.tensor_scalar(xf[:], at_tile(rows, t), mv2[:, 0:1], rstd2[:], ALU.subtract, ALU.mult).then_inc(xf_ready, 1)

            def xfT_low(t):
                dve.wait_ge(xfT_hi_ready, t + 1)
                nc.vector.tensor_tensor(flat(xfT_lo), H_ps[0][:], flat(xfT_hi).bitcast(f32), ALU.subtract).then_inc(xfT_lo_ready, 1)

            def t_low(t):
                dve.wait_ge(t_hi_ready, t + 1)
                for rs in (slice(P // 4, P // 2), slice(3 * P // 4, P)):
                    last = nc.vector.tensor_tensor(t_parts[rs, :], inter_ps[0][rs, 0:P], t_parts[rs, :].bitcast(f32), ALU.subtract)
                last.then_inc(t_ready, 1)

            def w1_low(k0, k1):
                for k in range(k0, k1):
                    ks = slice(k * P, (k + 1) * P)
                    dve.wait_ge(w1_hi_ready, k + 1)
                    nc.vector.tensor_tensor(w1T_lo[:, :, ks], chunks(H_ps[k % 2]), w1T_hi[:, :, ks].bitcast(f32), ALU.subtract
                                            ).then_inc(w1_lo_ready, 1)

            def w2_low(k0, k1):
                for k in range(k0, k1, 2):
                    dve.wait_ge(w2_hi_ready, k + 1)
                    nc.vector.tensor_tensor(w2_lo[:, k, :], w2_stage[:, k % W2_SLOTS, :], w2_hi[:, k, :].bitcast(f32), ALU.subtract
                                            ).then_inc(w2_lo_odd_ready, 1)

            def choose(t, g):
                find_max(t, g)
                scan(t, g)

            def find_max(t, g):
                w = GROUPS[g][1] * P
                n = t * NG + g
                dve.wait_ge(inter_done, n + 1)
                blocks = inter_ps[g % 2][:, 0:w].rearrange("p (b i) -> p b i", i=BLK)
                nc.vector.tensor_reduce(blk_max[:, 0:w // BLK], blocks, AX.X, ALU.max).then_inc(blk_max_ready, 1)
                dve.wait_ge(blk_max_ready, n + 1)
                nc.vector.tensor_tensor(is_max[:, 0:w].rearrange("p (b i) -> p b i", i=BLK), blocks,
                                        blk_max[:, 0:w // BLK].unsqueeze(2).to_broadcast([P, w // BLK, BLK]),
                                        ALU.is_equal).then_inc(is_max_ready, 1)

            def scan(t, g):
                w = GROUPS[g][1] * P
                n = t * NG + g
                dve.wait_ge(is_max_ready, n + 1)
                nc.vector.tensor_tensor_scan(first[:, g % 2, 0:w], doubling[:, 0:w], is_max[:, 0:w], 0.0,
                                             ALU.mult, ALU.add).then_inc(first_ready, 1)

            def mask(t, g):
                w = GROUPS[g][1] * P
                n = t * NG + g
                dve.wait_ge(H_done, n + 1)
                dve.wait_ge(first_ready, n + 1)
                nc.vector.scalar_tensor_tensor(h[:, g % 2, 0:w], first[:, g % 2, 0:w], 1.0, H_ps[g % 2][:, 0:w],
                                               ALU.is_equal, ALU.mult).then_inc(h_ready, 1)

            def hT_low(t, g):
                w = GROUPS[g][1] * P
                dve.wait_ge(hT_hi_ready, t * NG + g + 1)
                nc.vector.scalar_tensor_tensor(hT_lo[:, g % 2, 0:w], turn_ps[:, 0:w], 0.0, hT_hi[:, g % 2, 0:w].bitcast(f32),
                                               ALU.max, ALU.subtract).then_inc(hT_lo_ready, 1)

            def result(t):
                dve.wait_ge(ffn_done, t + 1)
                nc.vector.scalar_tensor_tensor(at_tile(rows, t), ffn_ps[:], tanh_g[:, 1:2], at_tile(rows, t),
                                               ALU.mult, ALU.add).then_inc(out_ready, 1)

            nc.vector.memset(W_bd[:], 0.0).then_inc(consts2_ready, 1)
            dve.wait_ge(consts2_ready, 3)
            dve.wait_ge(s_small, 16 * 4 * PAIR)
            for b in range(PAIR):
                rs = slice(b * C, (b + 1) * C)
                nc.vector.tensor_copy(W_bd[rs, :, b * C:(b + 1) * C], W_in[rs, :, :]).then_inc(W_bd_ready, 1)
            dve.wait_ge(s_c2, 16)
            for part in (0, 2):
                nc.vector.tensor_copy(c2_parts[:, 0:NF, part, :].bitcast(f32r), c2_raw[:]).then_inc(c2_parts_ready, 1)
            dve.wait_ge(c2_parts_ready, 1)
            for part in (1, 3):
                nc.vector.tensor_tensor(c2_parts[:, 0:NF, part, :], c2_raw[:], c2_parts[:, 0:NF, 0, :], ALU.subtract
                                        ).then_inc(c2_parts_ready, 1)
            dve.wait_ge(whi_ready, 1)
            nc.vector.scalar_tensor_tensor(G_lo[:], H_ps[0][:, 0:P], float(C) ** -0.5, G_hi[:].bitcast(f32),
                                           ALU.mult, ALU.subtract).then_inc(wlo_ready, 1)
            dve.wait_ge(whi_ready, 2)
            nc.vector.tensor_tensor(flat(WT_lo), H_ps[1][:, 0:2 * P], flat(WT_hi).bitcast(f32), ALU.subtract).then_inc(wlo_ready, 1)
            dve.wait_ge(consts_ready, CONSTS)
            AV_low(0)
            dve.wait_ge(c1_hi_ready, 1)
            nc.vector.tensor_tensor(c1T_parts[:, :, 1, :], chunks(turn_ps)[:, :, P // 2:P], c1T_parts[:, :, 0, :].bitcast(f32),
                                    ALU.subtract).then_inc(c1_lo_ready, 1)
            w1_low(0, 2)
            row_max(0)
            inv_sums(0)
            w1_low(2, 7)
            PT_low(0)
            dve.wait_ge(tanh_ready, 1)
            w1_low(7, NF)
            x2_step(0)
            w2_low(1, 6)
            xf_step(0)
            xfT_low(0)
            w2_low(7, 10)
            t_low(0)
            w2_low(11, NF)
            with dve.Fori(0, TILES - 1) as t:
                choose(t, 0)
                mask(t, 0)
                find_max(t, 1)
                AV_low(t + 1)
                hT_low(t, 0)
                scan(t, 1)
                mask(t, 1)
                row_max(t + 1)
                hT_low(t, 1)
                choose(t, 2)
                inv_sums(t + 1)
                mask(t, 2)
                PT_low(t + 1)
                choose(t, 3)
                hT_low(t, 2)
                mask(t, 3)
                x2_step(t + 1)
                xf_step(t + 1)
                hT_low(t, 3)
                xfT_low(t + 1)
                t_low(t + 1)
                result(t)
            t = TILES - 1
            choose(t, 0)
            choose(t, 1)
            for g in range(NG):
                mask(t, g)
                hT_low(t, g)
                if g + 2 < NG:
                    choose(t, g + 2)
            result(t)

        @block.tensor
        def _(pe):
            def AV(t):
                pe.wait_ge(ctx_lo_ready, t + 1)
                wait_past(pe, x2_ready, t)
                three_passes(att_ps[0][:, 0:M], G_hi[:], G_lo[:], ctx_hi[:], ctx_lo[:])
                three_passes(att_ps[0][:, M:2 * M], ctx_hi[:], ctx_lo[:], WT_hi[:, 0, :], WT_lo[:, 0, :]).then_inc(AV_done, 1)

            def energy(t):
                pe.wait_ge(AV_lo_ready, t + 1)
                pe.wait_ge(up_lo_ready, t + 1)
                for j in range(ND):
                    js = slice(j * P, (j + 1) * P)
                    cs = slice(j % 2 * PAIR * M, (j % 2 + 1) * PAIR * M)
                    last = three_passes(att_ps[j // 2][:, cs], up_hi[:, js], up_lo[:, js], A_hi[:], A_lo[:])
                last.then_inc(energy_done, 1)

            def turn_probs(t):
                pe.wait_ge(probs_ready, t * 2 + 2)
                for b in range(PAIR):
                    for j in range(ND):
                        last = nc.tensor.transpose(att_ps[b][:, j * P:(j + 1) * P], probs[:, j, b, :], ident[:])
                    last.then_inc(probs_turned, 1)

            def xattn(t):
                pe.wait_ge(PT_lo_ready, t * 2 + 1)
                three_passes(att_ps[0][:], WT_hi[:, 1, :], WT_lo[:, 1, :], up_hi[:], up_lo[:], True, False)
                for b in range(PAIR):
                    pe.wait_ge(PT_lo_ready, t * 2 + b + 1)
                    vs = slice(PAIR * b, PAIR * (b + 1))
                    last = three_passes(att_ps[0][:], flat2(v_hi[:, vs, :]), flat2(v_lo[:, vs, :]), PT_hi[:, b, :], PT_lo[:, b, :],
                                        False, b == PAIR - 1)
                last.then_inc(xattn_done, 1)

            def turn_xf(t):
                pe.wait_ge(xf_ready, t + 1)
                for d in range(ND):
                    last = nc.tensor.transpose(H_ps[0][:, d * P:(d + 1) * P], xf[:, d * P:(d + 1) * P], ident[:])
                last.then_inc(xf_turned, 1)

            def low_rank(t):
                pe.wait_ge(xfT_lo_ready, t + 1)
                for d in range(ND):
                    c1 = flat2(c1T_parts[:, d, :, :])
                    nc.tensor.matmul(inter_ps[0][:, 0:P], c1, xfT_hi[:, d, :], start=d == 0, stop=False)
                    last = nc.tensor.matmul(inter_ps[0][:, 0:P], c1, xfT_lo[:, d, :], start=False, stop=d == ND - 1)
                last.then_inc(t_done, 1)

            def inter(t, g):
                k0, n = GROUPS[g]
                if g == 0:
                    pe.wait_ge(t_ready, t + 1)
                if g >= 2:
                    pe.wait_ge(is_max_ready, t * NG + g - 1)
                nc.tensor.matmul(inter_ps[g % 2][:, 0:n * P], t_parts[:], c2T[:, k0 * P:(k0 + n) * P],
                                 start=True, stop=True).then_inc(inter_done, 1)

            def H(t, g):
                k0, n = GROUPS[g]
                fs = slice(k0 * P, (k0 + n) * P)
                if g >= 2:
                    pe.wait_ge(h_ready, t * NG + g - 1)
                for d in range(ND):
                    last = three_passes(H_ps[g % 2][:, 0:n * P], xfT_hi[:, d, :], xfT_lo[:, d, :], w1T_hi[:, d, fs], w1T_lo[:, d, fs],
                                        d == 0, d == ND - 1)
                last.then_inc(H_done, 1)

            def turn_h(t, g):
                pe.wait_ge(h_ready, t * NG + g + 1)
                if g >= 1:
                    pe.wait_ge(hT_lo_ready, t * NG + g)
                for k in range(GROUPS[g][1]):
                    ks = slice(k * P, (k + 1) * P)
                    last = nc.tensor.transpose(turn_ps[:, ks], h[:, g % 2, ks], ident[:])
                last.then_inc(h_turned, 1)

            def down(t, g):
                k0, n = GROUPS[g]
                pe.wait_ge(hT_lo_ready, t * NG + g + 1)
                pe.wait_ge(w2_lo_even_ready, (k0 + n) // 2)
                pe.wait_ge(w2_lo_odd_ready, (k0 + n) // 2)
                for k in range(n):
                    ks = slice(k * P, (k + 1) * P)
                    last = three_passes(ffn_ps[:], hT_hi[:, g % 2, ks], hT_lo[:, g % 2, ks], w2_hi[:, k0 + k, :], w2_lo[:, k0 + k, :],
                                        k0 + k == 0, k0 + k == NF - 1)
                if g == NG - 1:
                    last.then_inc(ffn_done, 1)

            def turn_w1(k0, k1):
                for k in range(k0, k1):
                    slot = k % W1_SLOTS
                    pe.wait_ge(s_w1[slot], 16 * (k // W1_SLOTS + 1))
                    if k >= 2:
                        pe.wait_ge(w1_lo_ready, k - 1)
                    for d in range(ND):
                        last = nc.tensor.transpose(H_ps[k % 2][:, d * P:(d + 1) * P], rows[:, 1 + slot, d * P:(d + 1) * P], ident[:])
                    last.then_inc(w1_turned, 1)

            pe.wait_ge(ident_ready, 1)
            pe.wait_ge(W_bd_ready, 2)
            nc.tensor.matmul(H_ps[0][:, 0:P], W_bd[:, 0, :], W_bd[:, 1, :], start=True, stop=True).then_inc(wprod_ready, 1)
            for n in range(2):
                last = nc.tensor.transpose(H_ps[1][:, n * P:(n + 1) * P], W_bd[:, 2 + n, :], ident[:])
            last.then_inc(wprod_ready, 1)
            pe.wait_ge(wlo_ready, 2)
            AV(0)
            pe.wait_ge(s_c1, 16 * REP)
            for d in range(ND):
                last = nc.tensor.transpose(turn_ps[:, d * P:(d + 1) * P], c1_rep[:, d * P:(d + 1) * P], ident[:])
            last.then_inc(c1_turned, 1)
            turn_w1(0, 2)
            energy(0)
            turn_w1(2, 7)
            pe.wait_ge(c2_parts_ready, 4)
            pe.wait_ge(consts_ready, CONSTS)
            for g, (k0, n) in enumerate(GROUPS):
                if g >= 2:
                    pe.wait_ge(c2_ready, g - 1)
                for k in range(n):
                    last = nc.tensor.transpose(inter_ps[g % 2][:, k * P:(k + 1) * P],
                                               c2_parts[:, k0 + k:k0 + k + 2, :, :].rearrange("p k a r -> p (k a r)"), ident[:])
                last.then_inc(c2_turned, 1)
            turn_probs(0)
            turn_w1(7, 10)
            xattn(0)
            turn_w1(10, NF)
            pe.wait_ge(w1_lo_ready, NF)
            turn_xf(0)
            pe.wait_ge(c1_lo_ready, 1)
            pe.wait_ge(c2_ready, NG)
            low_rank(0)
            with pe.Fori(0, TILES - 1) as t:
                inter(t, 0)
                inter(t, 1)
                H(t, 0)
                AV(t + 1)
                turn_h(t, 0)
                H(t, 1)
                inter(t, 2)
                energy(t + 1)
                turn_h(t, 1)
                inter(t, 3)
                down(t, 0)
                H(t, 2)
                turn_probs(t + 1)
                turn_h(t, 2)
                H(t, 3)
                xattn(t + 1)
                down(t, 1)
                turn_h(t, 3)
                turn_xf(t + 1)
                down(t, 2)
                low_rank(t + 1)
                down(t, 3)
            t = TILES - 1
            inter(t, 0)
            inter(t, 1)
            H(t, 0)
            H(t, 1)
            for g in range(NG):
                turn_h(t, g)
                if g + 2 < NG:
                    inter(t, g + 2)
                    H(t, g + 2)
                down(t, g)


_INS = ['x', 'ctx_1024', 'g_xattn', 'g_ffn', 'L0_xattn_Wq', 'L0_xattn_Wk', 'L0_xattn_Wv', 'L0_xattn_Wskip',
        'L0_ffn_c1_w', 'L0_ffn_c2_w', 'L0_ffn_w1', 'L0_ffn_w2t']


def kernel(**inputs):
    import numpy as np
    import concourse.bacc as bacc
    from concourse.bass_utils import run_bass_kernel_spmd

    nc = bacc.Bacc("TRN2", target_bir_lowering=False, num_devices=1)
    arrays, args = {}, []
    for name in _INS:
        a = np.ascontiguousarray(inputs[name])
        arrays[f"in_{name}"] = a
        args.append(nc.dram_tensor(f"in_{name}", a.shape, mybir.dt.from_np(a.dtype), kind="ExternalInput").ap())
    x = arrays["in_x"]
    args.append(nc.dram_tensor("out", x.shape, mybir.dt.from_np(x.dtype), kind="ExternalOutput").ap())
    flamingo_gated_layer(nc, *args)
    r = run_bass_kernel_spmd(nc, [arrays], core_ids=[0])
    return r.results[0]["out"]
```

```python
import concourse.bass as bass
from concourse import mybir
from contextlib import ExitStack


def flamingo_gated_layer(
    nc: bass.Bass,
    x: bass.AP,
    ctx: bass.AP,
    g_xattn: bass.AP,
    g_ffn: bass.AP,
    Wq: bass.AP,
    Wk: bass.AP,
    Wv: bass.AP,
    Wskip: bass.AP,
    c1_w: bass.AP,
    c2_w: bass.AP,
    w1: bass.AP,
    w2t: bass.AP,
    out: bass.AP,
):
    f32 = mybir.dt.float32
    f32r = mybir.dt.float32r
    bf16 = mybir.dt.bfloat16
    ALU = mybir.AluOpType
    ACT = mybir.ActivationFunctionType
    AX = mybir.AxisListType

    P = 128
    B, C, N = x.shape
    M = ctx.shape[2]
    R = c1_w.shape[0]
    F = w1.shape[0]
    BLK = 32
    TILES = B * C // P
    PAIR = P // C
    ND = N // P
    NF = F // P
    GF = 4
    GROUPS = [(g, min(GF, NF - g)) for g in range(0, NF, GF)]
    NG = len(GROUPS)
    GW = GF * P
    EPS = 1e-5
    W1_SLOTS = TILES
    W2_SLOTS = 4
    W2_POOL = 3
    W1_POOL = 2

    x_rows = x.rearrange("(t b) c n -> (b c) t n", b=PAIR)
    out_rows = out.rearrange("(t b) c n -> (b c) t n", b=PAIR)
    ctx_rows = ctx.rearrange("(t b) c m -> (b c) t m", b=PAIR)
    w1_rows = w1.rearrange("(k p) n -> p k n", p=P)
    w2_rows = w2t.rearrange("(k p) n -> p k n", p=P)
    c2_rows = c2_w.rearrange("(k p) r -> p k r", p=P)

    stack = ExitStack()
    with stack:
        def sb(name, shape, dt=f32):
            return stack.enter_context(nc.sbuf_tensor(name, shape, dt))

        def bank(name):
            return stack.enter_context(nc.psum_tensor(name, [P, 512], f32))

        def sem(name):
            return stack.enter_context(nc.semaphore(name))

        w1T_hi = sb("w1T_hi", [P, ND, F], f32r)
        w1T_lo = sb("w1T_lo", [P, ND, F], f32r)
        w2_hi = sb("w2_hi", [P, NF, N], f32r)
        w2_lo = sb("w2_lo", [P, NF, N], f32r)
        c2T = sb("c2T", [P, F], f32r)
        c1T_parts = sb("c1T_parts", [P, ND, P // 2 // R, 2, R], f32r)
        G_hi = sb("G_hi", [P, P], f32r)
        G_lo = sb("G_lo", [P, P], f32r)
        WT = sb("WT", [P, 2, 2, P], f32r)
        WT_hi, WT_lo = WT[:, :, 0, :], WT[:, :, 1, :]
        ident = sb("ident", [P, P])
        doubling = sb("doubling", [P, GW], bf16)
        minus_half = sb("minus_half", [P, 1])
        eps = sb("eps", [P, 1])
        over_n = sb("over_n", [P, 1])
        minus_over_n = sb("minus_over_n", [P, 1])
        gates = sb("gates", [P, 2])
        tanh_g = sb("tanh_g", [P, 2])
        W_in = sb("W_in", [C, 4, C])
        W_bd = sb("W_bd", [P, 4, P])
        c2_raw = sb("c2_raw", [P, NF, R])
        w2_stage = sb("w2_stage", [P, W2_SLOTS, N])
        rows = sb("rows", [P, TILES, N])
        x_sum = sb("x_sum", [P, 1])
        neg_mean = sb("neg_mean", [P, 1])
        square_sum = sb("square_sum", [P, 1])
        var_eps = sb("var_eps", [P, 1])
        rstd1 = sb("rstd1", [P, 1])
        centred = sb("centred", [P, N])
        up = sb("up", [P, N])
        up_hi = sb("up_hi", [P, N], f32r)
        up_lo = sb("up_lo", [P, N], f32r)
        ctx_all = sb("ctx_all", [P, TILES, M])
        ctx_parts = sb("ctx_parts", [P, 2, M], f32r)
        ctx_hi, ctx_lo = ctx_parts[:, 0, :], ctx_parts[:, 1, :]
        A_hi = sb("A_hi", [P, PAIR * M], f32r)
        A_lo = sb("A_lo", [P, PAIR * M], f32r)
        v_hi = sb("v_hi", [P, 2 * PAIR, C], f32r)
        v_lo = sb("v_lo", [P, 2 * PAIR, C], f32r)
        neg_max = sb("neg_max", [P, ND * PAIR])
        row_sum = sb("row_sum", [P, ND * PAIR])
        inv_sum = sb("inv_sum", [P, ND * PAIR])
        probs = sb("probs", [P, ND, PAIR, M])
        PT_hi = sb("PT_hi", [P, 2, PAIR, N // 2], f32r)
        PT_lo = sb("PT_lo", [P, 2, PAIR, N // 2], f32r)
        stats2 = sb("stats2", [P, 6])
        mv2 = sb("mv2", [P, 2])
        rstd2 = sb("rstd2", [P, 1])
        xf = sb("xf", [P, N])
        xfT = sb("xfT", [P, ND, 2, P], f32r)
        xfT_hi, xfT_lo = xfT[:, :, 0, :], xfT[:, :, 1, :]
        t_parts = sb("t_parts", [P, P], f32r)
        blk_max = sb("blk_max", [P, GW // BLK])
        is_max = sb("is_max", [P, GW], bf16)
        first = sb("first", [P, 2, GW], bf16)
        h = sb("h", [P, 2, GW])
        hT_hi = sb("hT_hi", [P, 2, GW], f32r)
        hT_lo = sb("hT_lo", [P, 2, GW], f32r)
        c1_in = xf
        w1_raw = probs[:].rearrange("p j b m -> p (j b m)").rearrange("p (k d f) -> p k d f", k=W1_POOL, d=ND)
        w1_stage = [rows[:, 2 + n, :] for n in range(TILES - 2)] + [h[:, n, :] for n in range(2)]
        c2_parts = w2_hi[:, NF // 2:, :].rearrange("p a b -> p (a b)")[:, 0:NF * P].rearrange("p (k a r) -> p k a r", a=P // R, r=R)

        inter_ps = [bank("inter0"), bank("inter1")]
        H_ps = [bank("H0"), bank("H1")]
        turn_ps = bank("turn")
        ffn_ps = bank("ffn")
        att_ps = [bank("att0"), bank("att1")]
        w1_banks = [H_ps[0], H_ps[1], turn_ps, H_ps[0], H_ps[1], turn_ps, att_ps[1], ffn_ps, H_ps[1], turn_ps,
                    att_ps[1], ffn_ps, turn_ps, att_ps[1]]

        s_x = [sem("x0_in"), sem("x1_in"), sem("xrest_in")]
        s_KQ = sem("Wk_Wq_in")
        s_VS = sem("Wv_Wskip_in")
        s_c1 = sem("c1_in")
        s_c2 = sem("c2_in")
        s_g = sem("gates_in")
        s_ctx = [sem("ctx0_in"), sem("ctxrest_in")]
        s_w1 = [sem(f"w1_slot{n}_in") for n in range(W1_SLOTS)]
        s_w2 = [sem(f"w2_slot{n}_in") for n in range(W2_SLOTS)]
        s_out = sem("out_written")
        zeroed = sem("zeroed")
        ident_ready = sem("ident_ready")
        consts_ready = sem("consts_ready")
        tanh_ready = sem("tanh_ready")
        wprod_ready = sem("wprod_ready")
        whi_ready = sem("whi_ready")
        wlo_ready = sem("wlo_ready")
        w1_turned = sem("w1_turned")
        w1_hi_ready = sem("w1_hi_ready")
        w1_lo_ready = sem("w1_lo_ready")
        w1_raw_ready = sem("w1_raw_ready")
        w1_pool_lo_ready = sem("w1_pool_lo_ready")
        W_bd_ready = sem("W_bd_ready")
        w2_hi_ready = sem("w2_hi_ready")
        w2_lo_ready = sem("w2_lo_ready")
        w2_pool_hi_ready = sem("w2_pool_hi_ready")
        c1_turned = sem("c1_turned")
        c1_hi_ready = sem("c1_hi_ready")
        c1_lo_ready = sem("c1_lo_ready")
        c2_parts_ready = sem("c2_parts_ready")
        c2_turned = sem("c2_turned")
        c2_ready = sem("c2_ready")
        consts2_ready = sem("consts2_ready")

        x_sum_ready = sem("x_sum_ready")
        neg_mean_ready = sem("neg_mean_ready")
        centred_ready = sem("centred_ready")
        square_sum_ready = sem("square_sum_ready")
        rstd1_ready = sem("rstd1_ready")
        up_ready = sem("up_ready")
        up_hi_ready = sem("up_hi_ready")
        up_lo_ready = sem("up_lo_ready")
        ctx_hi_ready = sem("ctx_hi_ready")
        ctx_lo_ready = sem("ctx_lo_ready")
        x0_stats_ready = sem("x0_stats_ready")
        x0_mv_ready = sem("x0_mv_ready")
        x0_var_ready = sem("x0_var_ready")
        A0_done = sem("A0_done")
        A0_hi_ready = sem("A0_hi_ready")
        A0_lo_ready = sem("A0_lo_ready")
        AV_rest_ready = sem("AV_rest_ready")
        AV_done = sem("AV_done")
        AV_hi_ready = sem("AV_hi_ready")
        AV_lo_ready = sem("AV_lo_ready")
        c1_zeroed = sem("c1_zeroed")
        energy_done = sem("energy_done")
        neg_max_ready = sem("neg_max_ready")
        exp_ready = sem("exp_ready")
        inv_sum_ready = sem("inv_sum_ready")
        probs_ready = sem("probs_ready")
        probs_turned = sem("probs_turned")
        PT_hi_ready = sem("PT_hi_ready")
        PT_lo_ready = sem("PT_lo_ready")
        xattn_done = sem("xattn_done")
        x2_ready = sem("x2_ready")
        stats2_ready = sem("stats2_ready")
        mv2_ready = sem("mv2_ready")
        var1_ready = sem("var1_ready")
        var2_ready = sem("var2_ready")
        rstd2_ready = sem("rstd2_ready")
        xf_ready = sem("xf_ready")
        xf_turned = sem("xf_turned")
        xfT_hi_ready = sem("xfT_hi_ready")
        xfT_lo_ready = sem("xfT_lo_ready")
        t_done = sem("t_done")
        t_hi_ready = sem("t_hi_ready")
        t_lo_ready = sem("t_lo_ready")
        t_rest_ready = sem("t_rest_ready")
        inter_done = sem("inter_done")
        blk_max_ready = sem("blk_max_ready")
        is_max_ready = sem("is_max_ready")
        first_ready = sem("first_ready")
        H_done = sem("H_done")
        h_ready = sem("h_ready")
        h_turned = sem("h_turned")
        hT_hi_ready = sem("hT_hi_ready")
        hT_lo_ready = sem("hT_lo_ready")
        ffn_done = sem("ffn_done")
        out_ready = sem("out_ready")

        CONSTS = 8

        def xf_bank(t):
            return att_ps[0] if isinstance(t, int) and t == 0 else H_ps[0]

        def v_ps(t):
            return ffn_ps[:, 0:2 * M] if isinstance(t, int) and t == 0 else att_ps[0][:, 2 * M:4 * M]

        def h_turn_bank(t, g):
            if isinstance(t, int) and t == TILES - 1:
                return [turn_ps, att_ps[0], att_ps[1], turn_ps][g]
            return turn_ps

        def flat(ap):
            return ap.rearrange("p a b -> p (a b)")

        def chunks(ps):
            return ps[:].rearrange("p (d f) -> p d f", d=ND)

        def at_tile(buf, t):
            return buf[:, bass.ds(t, 1), :].rearrange("p o w -> p (o w)")

        def three_passes(ps, lhs_hi, lhs_lo, rhs_hi, rhs_lo, start=True, stop=True):
            nc.tensor.matmul(ps, lhs_hi, rhs_hi, start=start, stop=False)
            nc.tensor.matmul(ps, lhs_hi, rhs_lo, start=False, stop=False)
            return nc.tensor.matmul(ps, lhs_lo, rhs_hi, start=False, stop=stop)

        c1_turned_rep = inter_ps[0][:, 0:ND * R].rearrange("p (d r) -> p d r", r=R).unsqueeze(2).to_broadcast([P, ND, P // 2 // R, R])

        block = stack.enter_context(nc.Block())

        @block.sync
        def _(sp):
            sp.dma_start(rows[:, 0, :], x_rows[:, 0, :]).then_inc(s_x[0], 16)
            for n, w in enumerate((Wk, Wq, Wv, Wskip)):
                sp.dma_start(W_in[:, n, :], w).then_inc(s_KQ if n < 2 else s_VS, 16)
                if n == 1:
                    sp.dma_start(ctx_all[:, 0, :], ctx_rows[:, 0, :]).then_inc(s_ctx[0], 16)
            sp.dma_start(c2_raw[:], c2_rows).then_inc(s_c2, 16)
            sp.wait_ge(c1_zeroed, 1)
            sp.dma_start(c1_in[0:R, :], c1_w).then_inc(s_c1, 16)

            def load_w1(k0, k1):
                for k in range(k0, k1):
                    slot = k % W1_SLOTS
                    if k >= W1_SLOTS:
                        sp.wait_ge(w1_turned, k - W1_SLOTS + 1)
                    sp.dma_start(w1_stage[slot], w1_rows[:, k, :]).then_inc(s_w1[slot], 16)

            def load_w2(k0, k1):
                for k in range(k0, k1):
                    slot = k % W2_SLOTS
                    if k >= W2_SLOTS:
                        sp.wait_ge(w2_lo_ready, k - W2_SLOTS + 1)
                    sp.dma_start(w2_stage[:, slot, :], w2_rows[:, k, :]).then_inc(s_w2[slot], 16)

            load_w1(0, 1)
            sp.dma_start(gates[:, 0:1], g_xattn.unsqueeze(0).to_broadcast([P, 1])).then_inc(s_g, 16)
            sp.dma_start(gates[:, 1:2], g_ffn.unsqueeze(0).to_broadcast([P, 1])).then_inc(s_g, 16)
            load_w1(1, 4)
            load_w2(0, W2_POOL)
            load_w1(4, W1_SLOTS)
            load_w2(W2_POOL, W2_SLOTS)
            sp.dma_start(rows[:, 1, :], x_rows[:, 1, :]).then_inc(s_x[1], 16)
            sp.dma_start(ctx_all[:, 1:, :], ctx_rows[:, 1:, :]).then_inc(s_ctx[1], 16)
            load_w1(W1_SLOTS, 11)
            load_w2(4, 6)
            load_w1(11, NF)
            load_w2(6, NF)
            sp.wait_ge(w1_turned, NF)
            sp.dma_start(rows[:, 2:, :], x_rows[:, 2:, :]).then_inc(s_x[2], 16)
            with sp.Fori(0, TILES - 1) as t:
                sp.wait_ge(out_ready, t + 1)
                sp.dma_start(out_rows[:, bass.ds(t, 1), :], rows[:, bass.ds(t, 1), :]).then_inc(s_out, 16)
            for half in range(2):
                sp.wait_ge(out_ready, TILES + half)
                cs = slice(half * N // 2, (half + 1) * N // 2)
                sp.dma_start(out_rows[:, TILES - 1, cs], rows[:, TILES - 1, cs]).then_inc(s_out, 16)
            sp.wait_ge(s_out, 16 * (TILES + 1))

        @block.gpsimd
        def _(pool):
            nc.gpsimd.memset(ident[:], 0.0).then_inc(zeroed, 1)
            nc.gpsimd.memset(minus_half[:], -0.5).then_inc(consts_ready, 1)
            nc.gpsimd.memset(eps[:], EPS).then_inc(consts_ready, 1)
            nc.gpsimd.memset(over_n[:], 1.0 / N).then_inc(consts_ready, 1)
            nc.gpsimd.memset(minus_over_n[:], -1.0 / N).then_inc(consts_ready, 1)
            for buf in (A_hi[:], A_lo[:], v_hi[:], v_lo[:]):
                nc.gpsimd.memset(buf.bitcast(f32), 0.0).then_inc(consts_ready, 1)
            pool.wait_ge(zeroed, 1)
            nc.gpsimd.affine_select(out=ident[:], in_=ident[:], compare_op=ALU.not_equal, fill=1.0, base=0,
                                    pattern=[[-1, P]], channel_multiplier=1).then_inc(ident_ready, 1)

            def mean1(t):
                pool.wait_ge(x_sum_ready, t)
                nc.gpsimd.tensor_tensor(neg_mean[:], x_sum[:], minus_over_n[:], ALU.mult).then_inc(neg_mean_ready, 1)

            def rstd1_step(t):
                pool.wait_ge(square_sum_ready, t)
                nc.gpsimd.tensor_tensor(var_eps[:], square_sum[:], over_n[:], ALU.mult).then_inc(var1_ready, 1)
                pool.wait_ge(var1_ready, t * 2 - 1)
                nc.gpsimd.tensor_tensor(var_eps[:], var_eps[:], eps[:], ALU.add).then_inc(var1_ready, 1)
                pool.wait_ge(var1_ready, t * 2)
                nc.gpsimd.tensor_tensor(rstd1[:], var_eps[:], minus_half[:], ALU.pow).then_inc(rstd1_ready, 1)

            def ctx_low(t):
                pool.wait_ge(ctx_hi_ready, t + 1)
                nc.gpsimd.tensor_tensor(ctx_lo, at_tile(ctx_all, t), ctx_hi.bitcast(f32), ALU.subtract).then_inc(ctx_lo_ready, 1)

            def rstd2_step(t):
                pool.wait_ge(mv2_ready, t + 1)
                nc.gpsimd.tensor_tensor(rstd2[:], mv2[:, 1:2], eps[:], ALU.add).then_inc(var2_ready, 1)
                pool.wait_ge(var2_ready, t + 1)
                nc.gpsimd.tensor_tensor(rstd2[:], rstd2[:], minus_half[:], ALU.pow).then_inc(rstd2_ready, 1)

            def up_low(t):
                pool.wait_ge(up_hi_ready, t + 1)
                nc.gpsimd.tensor_tensor(up_lo[:], up[:], up_hi[:].bitcast(f32), ALU.subtract).then_inc(up_lo_ready, 1)

            def normalise(t):
                for half in range(2):
                    pool.wait_ge(inv_sum_ready, t * 2 + half + 1)
                    js = slice(half * ND // 2, (half + 1) * ND // 2)
                    cols = slice(half * ND * PAIR // 2, (half + 1) * ND * PAIR // 2)
                    pr = probs[:, js, :, :].rearrange("p j b m -> p (j b) m")
                    nc.gpsimd.tensor_tensor(pr, pr, inv_sum[:, cols].unsqueeze(2).to_broadcast([P, ND * PAIR // 2, M]),
                                            ALU.mult).then_inc(probs_ready, 1)

            def w2_low(k0, k1):
                for k in range(k0, k1):
                    if k < W2_POOL:
                        pool.wait_ge(s_w2[k], 16)
                        nc.gpsimd.tensor_copy(w2_hi[:, k, :], w2_stage[:, k, :]).then_inc(w2_pool_hi_ready, 1)
                        pool.wait_ge(w2_pool_hi_ready, k + 1)
                    else:
                        pool.wait_ge(w2_hi_ready, k - W2_POOL + 1)
                    nc.gpsimd.tensor_tensor(w2_lo[:, k, :], w2_stage[:, k % W2_SLOTS, :], w2_hi[:, k, :].bitcast(f32),
                                            ALU.subtract).then_inc(w2_lo_ready, 1)

            pool.wait_ge(consts_ready, CONSTS)
            pool.wait_ge(x0_mv_ready, 1)
            nc.gpsimd.tensor_tensor(var_eps[:], mv2[:, 1:2], eps[:], ALU.add).then_inc(x0_var_ready, 1)
            pool.wait_ge(x0_var_ready, 1)
            nc.gpsimd.tensor_tensor(rstd1[:], var_eps[:], minus_half[:], ALU.pow).then_inc(rstd1_ready, 1)
            ctx_low(0)
            pool.wait_ge(s_c2, 16)
            nc.gpsimd.tensor_copy(c2_parts[:, :, 2:, :], c2_raw[:].unsqueeze(2).to_broadcast([P, NF, P // R - 2, R])
                                  ).then_inc(c2_parts_ready, 1)
            pool.wait_ge(c2_parts_ready, 1)
            nc.gpsimd.tensor_tensor(c2_parts[:, :, 0:2, :], c2_raw[:].unsqueeze(2).to_broadcast([P, NF, 2, R]),
                                    c2_parts[:, :, 2:4, :].bitcast(f32), ALU.subtract).then_inc(c2_parts_ready, 1)
            w2_low(0, 2)
            rstd2_step(0)

            def body(t):
                first_tile = isinstance(t, int)
                ctx_low(t + 1)
                mean1(t + 1)
                if first_tile:
                    w2_low(2, W2_POOL)
                rstd1_step(t + 1)
                up_low(t + 1)
                if first_tile:
                    for n in range(W1_POOL):
                        pool.wait_ge(w1_raw_ready, n + 1)
                        ks = slice((NF - W1_POOL + n) * P, (NF - W1_POOL + n + 1) * P)
                        nc.gpsimd.tensor_tensor(w1T_lo[:, :, ks], w1_raw[:, n, :, :], w1T_hi[:, :, ks].bitcast(f32), ALU.subtract
                                                ).then_inc(w1_pool_lo_ready, 1)
                    w2_low(W2_POOL, 6)
                normalise(t + 1)
                if first_tile:
                    w2_low(6, 12)
                rstd2_step(t + 1)
                if first_tile:
                    w2_low(12, NF)

            body(0)
            with pool.Fori(1, TILES - 1) as t:
                body(t)

        @block.scalar
        def _(act):
            def mean(t):
                nc.scalar.activation(centred[:], at_tile(rows, t), ACT.Copy, accum_out=x_sum[:]).then_inc(x_sum_ready, 1)
                ctx_high(t)

            def centre(t):
                act.wait_ge(neg_mean_ready, t)
                nc.scalar.activation(centred[:], centred[:], ACT.Identity, bias=neg_mean[:]).then_inc(centred_ready, 1)
                act.wait_ge(centred_ready, t)
                nc.scalar.activation(up[:], centred[:], ACT.Square, accum_out=square_sum[:]).then_inc(square_sum_ready, 1)

            def norm1(t):
                act.wait_ge(rstd1_ready, t + 1)
                nc.scalar.activation(up[:], centred[:], ACT.Copy, scale=rstd1[:]).then_inc(up_ready, 1)
                act.wait_ge(up_ready, t + 1)
                nc.scalar.activation(up_hi[:], up[:], ACT.Copy).then_inc(up_hi_ready, 1)

            def ctx_high(t):
                if isinstance(t, int):
                    act.wait_ge(s_ctx[min(t, 1)], 16)
                nc.scalar.activation(ctx_hi, at_tile(ctx_all, t), ACT.Copy).then_inc(ctx_hi_ready, 1)

            def A_high():
                for b in range(PAIR):
                    rs = slice(b * C, (b + 1) * C)
                    last = nc.scalar.activation(A_hi[rs, b * M:(b + 1) * M], att_ps[0][rs, 0:M], ACT.Copy)
                return last

            def v_high(t):
                nc.scalar.activation(v_hi[:, 0:2 * PAIR:PAIR + 1, :], v_ps(t)[:, 0:M].rearrange("p (b c) -> p b c", b=PAIR),
                                     ACT.Copy).then_inc(AV_hi_ready, 1)

            def AV_high(t):
                act.wait_ge(AV_done, t + 1)
                A_high()
                v_high(t)

            def exps(t):
                for half in range(2):
                    act.wait_ge(neg_max_ready, t * 2 + half + 1)
                    for jj in range(ND // 2):
                        for b in range(PAIR):
                            j = half * ND // 2 + jj
                            col = j * PAIR + b
                            at = (jj * PAIR + b) * M
                            last = nc.scalar.activation(probs[:, j, b, :], att_ps[half][:, at:at + M], ACT.Exp,
                                                        bias=neg_max[:, col:col + 1],
                                                        accum_out=row_sum[:, col:col + 1])
                    last.then_inc(exp_ready, 1)

            def PT_high_half(t, half):
                act.wait_ge(probs_turned, t * 2 + half + 1)
                nc.scalar.activation(flat(PT_hi[:, half, :, :]), att_ps[half][:], ACT.Copy).then_inc(PT_hi_ready, 1)

            def PT_high(t):
                PT_high_half(t, 0)
                PT_high_half(t, 1)

            def xfT_high(t):
                act.wait_ge(xf_turned, t + 1)
                nc.scalar.activation(xfT_hi, chunks(xf_bank(t)), ACT.Copy).then_inc(xfT_hi_ready, 1)

            def t_high(t):
                act.wait_ge(t_done, t + 1)
                nc.scalar.activation(t_parts[0:3 * P // 4, :], inter_ps[0][0:3 * P // 4, 0:P], ACT.Copy).then_inc(t_hi_ready, 1)
                nc.scalar.activation(t_parts[3 * P // 4:, :], inter_ps[0][3 * P // 4:, P:2 * P], ACT.Copy).then_inc(t_rest_ready, 1)

            def hT_high(t, g):
                w = GROUPS[g][1] * P
                act.wait_ge(h_turned, t * NG + g + 1)
                nc.scalar.activation(hT_hi[:, g % 2, 0:w], h_turn_bank(t, g)[:, 0:w], ACT.Relu).then_inc(hT_hi_ready, 1)

            def w1_high(k0, k1):
                for k in range(k0, k1):
                    act.wait_ge(w1_turned, k + 1)
                    nc.scalar.activation(w1T_hi[:, :, k * P:(k + 1) * P], chunks(w1_banks[k]), ACT.Copy).then_inc(w1_hi_ready, 1)

            def w1_high_raw(k):
                w1_high(k, k + 1)
                nc.scalar.activation(w1_raw[:, k - NF + W1_POOL, :, :], chunks(w1_banks[k]), ACT.Copy).then_inc(w1_raw_ready, 1)

            def w2_high(k0, k1):
                for k in range(k0, k1):
                    slot = k % W2_SLOTS
                    act.wait_ge(s_w2[slot], 16 * (k // W2_SLOTS + 1))
                    nc.scalar.activation(w2_hi[:, k, :], w2_stage[:, slot, :], ACT.Copy).then_inc(w2_hi_ready, 1)

            act.wait_ge(consts_ready, 2)
            nc.scalar.activation(tanh_g[:, 0:1], eps[:], ACT.Tanh).then_inc(tanh_ready, 1)
            ctx_high(0)
            act.wait_ge(wprod_ready, 1)
            nc.scalar.activation(G_hi[:], H_ps[0][:, 0:P], ACT.Copy, scale=float(C) ** -0.5).then_inc(whi_ready, 1)
            act.wait_ge(up_ready, 1)
            nc.scalar.activation(up_hi[:], up[:], ACT.Copy).then_inc(up_hi_ready, 1)
            act.wait_ge(consts_ready, CONSTS)
            act.wait_ge(A0_done, 1)
            A_high().then_inc(A0_hi_ready, 1)
            act.wait_ge(wprod_ready, 2)
            nc.scalar.activation(WT_hi, H_ps[1][:, 0:2 * P].rearrange("p (n c) -> p n c", n=2), ACT.Copy).then_inc(whi_ready, 1)

            def c2_copy(g):
                k0, n = GROUPS[g]
                act.wait_ge(c2_turned, g + 1)
                nc.scalar.activation(c2T[:, k0 * P:(k0 + n) * P], inter_ps[1 - g % 2][:, 0:n * P], ACT.Copy).then_inc(c2_ready, 1)

            w1_high(0, 1)
            act.wait_ge(s_g, 16 * 2)
            act.wait_ge(tanh_ready, 1)
            nc.scalar.activation(tanh_g[:], gates[:], ACT.Tanh).then_inc(tanh_ready, 1)
            exps(0)
            act.wait_ge(AV_done, 1)
            v_high(0)
            PT_high_half(0, 0)
            act.wait_ge(c1_turned, 1)
            nc.scalar.activation(c1T_parts[:, :, :, 0, :], c1_turned_rep, ACT.Copy).then_inc(c1_hi_ready, 1)
            w1_high(1, 2)
            PT_high_half(0, 1)
            c2_copy(0)
            w1_high(2, 4)
            c2_copy(1)
            w1_high(4, 8)
            act.wait_ge(s_x[1], 16)
            mean(1)
            c2_copy(2)
            xfT_high(0)
            c2_copy(3)
            w1_high(8, 9)
            centre(1)
            w1_high(9, 10)
            t_high(0)
            w1_high(10, NF - W1_POOL)
            norm1(1)
            w1_high_raw(NF - 2)

            def body(t):
                first_tile = isinstance(t, int)
                if not first_tile:
                    mean(t + 1)
                    centre(t + 1)
                AV_high(t + 1)
                if first_tile:
                    w1_high_raw(NF - 1)
                    w2_high(3, 4)
                else:
                    norm1(t + 1)
                hT_high(t, 0)
                if first_tile:
                    w2_high(4, 7)
                    act.wait_ge(w1_pool_lo_ready, W1_POOL)
                exps(t + 1)
                hT_high(t, 1)
                if first_tile:
                    w2_high(7, 10)
                PT_high(t + 1)
                hT_high(t, 2)
                if first_tile:
                    w2_high(10, NF)
                hT_high(t, 3)
                xfT_high(t + 1)
                t_high(t + 1)

            body(0)
            act.wait_ge(s_x[2], 16)
            with act.Fori(1, TILES - 1) as t:
                body(t)
            for g in range(NG):
                hT_high(TILES - 1, g)

        @block.vector
        def _(dve):
            nc.vector.memset(c1_in[:], 0.0).then_inc(c1_zeroed, 1)
            nc.vector.memset(doubling[:], 2.0).then_inc(consts2_ready, 1)
            dve.wait_ge(consts2_ready, 1)
            nc.vector.memset(doubling[:].rearrange("p (b i) -> p b i", i=BLK)[:, :, 0:1], 0.0).then_inc(consts2_ready, 1)

            def A_rest():
                for b in range(PAIR):
                    rs, cs = slice(b * C, (b + 1) * C), slice(b * M, (b + 1) * M)
                    last = nc.vector.tensor_tensor(A_lo[rs, cs], att_ps[0][rs, 0:M], A_hi[rs, cs].bitcast(f32), ALU.subtract)
                return last

            def v_rest(t):
                return nc.vector.tensor_tensor(v_lo[:, 0:2 * PAIR:PAIR + 1, :], v_ps(t)[:, 0:M].rearrange("p (b c) -> p b c", b=PAIR),
                                               v_hi[:, 0:2 * PAIR:PAIR + 1, :].bitcast(f32), ALU.subtract)

            def AV_low(t):
                dve.wait_ge(AV_hi_ready, t + 1)
                A_rest()
                v_rest(t).then_inc(AV_rest_ready, 1)
                dve.wait_ge(AV_rest_ready, t)
                for b in range(PAIR):
                    rs, cs = slice(b * C, (b + 1) * C), slice(b * M, (b + 1) * M)
                    nc.vector.tensor_tensor(A_lo[rs, cs], att_ps[0][rs, M:2 * M], A_lo[rs, cs].bitcast(f32), ALU.add)
                v_blocks = v_lo[:, 0:2 * PAIR:PAIR + 1, :]
                nc.vector.tensor_tensor(v_blocks, v_ps(t)[:, M:2 * M].rearrange("p (b c) -> p b c", b=PAIR),
                                        v_blocks.bitcast(f32), ALU.add).then_inc(AV_lo_ready, 1)

            def row_max(t, half):
                w = ND * PAIR // 2
                dve.wait_ge(energy_done, t * 2 + half + 1)
                nc.vector.tensor_reduce(neg_max[:, half * w:(half + 1) * w],
                                        att_ps[half][:].rearrange("p (k m) -> p k m", m=M), AX.X, ALU.max,
                                        negate=True).then_inc(neg_max_ready, 1)

            def inv_sums(t, half):
                w = ND * PAIR // 2
                dve.wait_ge(exp_ready, t * 2 + half + 1)
                nc.vector.reciprocal(inv_sum[:, half * w:(half + 1) * w], row_sum[:, half * w:(half + 1) * w]
                                     ).then_inc(inv_sum_ready, 1)

            def PT_low_half(t, half):
                dve.wait_ge(PT_hi_ready, t * 2 + half + 1)
                nc.vector.tensor_tensor(flat(PT_lo[:, half, :, :]), att_ps[half][:], flat(PT_hi[:, half, :, :]).bitcast(f32),
                                        ALU.subtract).then_inc(PT_lo_ready, 1)

            def PT_low(t):
                PT_low_half(t, 0)
                PT_low_half(t, 1)

            def x2_step(t):
                dve.wait_ge(xattn_done, t + 1)
                nc.vector.scalar_tensor_tensor(at_tile(rows, t), att_ps[0][:], tanh_g[:, 0:1], at_tile(rows, t),
                                               ALU.mult, ALU.add).then_inc(x2_ready, 1)
                dve.wait_ge(consts2_ready, 2)
                dve.wait_ge(x2_ready, t + 1)
                nc.vector.bn_stats(stats2[:], at_tile(rows, t)).then_inc(stats2_ready, 1)
                dve.wait_ge(consts2_ready, 2)
                dve.wait_ge(stats2_ready, t + 1)
                nc.vector.bn_aggr(mv2[:], stats2[:]).then_inc(mv2_ready, 1)

            def xf_step(t):
                dve.wait_ge(rstd2_ready, t + 1)
                nc.vector.tensor_scalar(xf[:], at_tile(rows, t), mv2[:, 0:1], rstd2[:], ALU.subtract, ALU.mult).then_inc(xf_ready, 1)

            def xfT_low(t):
                dve.wait_ge(xfT_hi_ready, t + 1)
                nc.vector.tensor_tensor(xfT_lo, chunks(xf_bank(t)), xfT_hi.bitcast(f32), ALU.subtract).then_inc(xfT_lo_ready, 1)

            def t_low(t):
                dve.wait_ge(t_hi_ready, t + 1)
                rs = slice(P // 2, 3 * P // 4)
                nc.vector.tensor_tensor(t_parts[rs, :], inter_ps[0][rs, 0:P], t_parts[rs, :].bitcast(f32), ALU.subtract
                                        ).then_inc(t_lo_ready, 1)

            def w1_low(k0, k1):
                for k in range(k0, k1):
                    ks = slice(k * P, (k + 1) * P)
                    dve.wait_ge(w1_hi_ready, k + 1)
                    nc.vector.tensor_tensor(w1T_lo[:, :, ks], chunks(w1_banks[k]), w1T_hi[:, :, ks].bitcast(f32), ALU.subtract
                                            ).then_inc(w1_lo_ready, 1)

            def choose(t, g):
                find_max(t, g)
                scan(t, g)

            def find_max(t, g):
                w = GROUPS[g][1] * P
                n = t * NG + g
                dve.wait_ge(inter_done, n + 1)
                blocks = inter_ps[g % 2][:, 0:w].rearrange("p (b i) -> p b i", i=BLK)
                nc.vector.tensor_reduce(blk_max[:, 0:w // BLK], blocks, AX.X, ALU.max).then_inc(blk_max_ready, 1)
                dve.wait_ge(blk_max_ready, n + 1)
                nc.vector.tensor_tensor(is_max[:, 0:w].rearrange("p (b i) -> p b i", i=BLK), blocks,
                                        blk_max[:, 0:w // BLK].unsqueeze(2).to_broadcast([P, w // BLK, BLK]),
                                        ALU.is_equal).then_inc(is_max_ready, 1)

            def scan(t, g):
                w = GROUPS[g][1] * P
                n = t * NG + g
                dve.wait_ge(is_max_ready, n + 1)
                nc.vector.tensor_tensor_scan(first[:, g % 2, 0:w], doubling[:, 0:w], is_max[:, 0:w], 0.0,
                                             ALU.mult, ALU.add).then_inc(first_ready, 1)

            def mask(t, g):
                w = GROUPS[g][1] * P
                n = t * NG + g
                dve.wait_ge(H_done, n + 1)
                dve.wait_ge(first_ready, n + 1)
                nc.vector.scalar_tensor_tensor(h[:, g % 2, 0:w], first[:, g % 2, 0:w], 1.0, H_ps[g % 2][:, 0:w],
                                               ALU.is_equal, ALU.mult).then_inc(h_ready, 1)

            def hT_low(t, g):
                w = GROUPS[g][1] * P
                dve.wait_ge(hT_hi_ready, t * NG + g + 1)
                nc.vector.scalar_tensor_tensor(hT_lo[:, g % 2, 0:w], h_turn_bank(t, g)[:, 0:w], 0.0, hT_hi[:, g % 2, 0:w].bitcast(f32),
                                               ALU.max, ALU.subtract).then_inc(hT_lo_ready, 1)

            def result(t):
                dve.wait_ge(ffn_done, t + 1)
                nc.vector.scalar_tensor_tensor(at_tile(rows, t), ffn_ps[:], tanh_g[:, 1:2], at_tile(rows, t),
                                               ALU.mult, ALU.add).then_inc(out_ready, 1)

            nc.vector.memset(W_bd[:], 0.0).then_inc(consts2_ready, 1)
            dve.wait_ge(consts2_ready, 3)
            dve.wait_ge(s_x[0], 16)
            nc.vector.bn_stats(stats2[:], rows[:, 0, :]).then_inc(x0_stats_ready, 1)

            def W_copy(n):
                for b in range(PAIR):
                    last = nc.vector.tensor_copy(W_bd[b * C:(b + 1) * C, n:n + 2, b * C:(b + 1) * C], W_in[:, n:n + 2, :])
                last.then_inc(W_bd_ready, 1)

            dve.wait_ge(x0_stats_ready, 1)
            nc.vector.bn_aggr(mv2[:], stats2[:]).then_inc(x0_mv_ready, 1)
            dve.wait_ge(s_KQ, 16 * 2)
            W_copy(0)
            dve.wait_ge(rstd1_ready, 1)
            nc.vector.tensor_scalar(up[:], rows[:, 0, :], mv2[:, 0:1], rstd1[:], ALU.subtract, ALU.mult).then_inc(up_ready, 1)
            dve.wait_ge(whi_ready, 1)
            nc.vector.scalar_tensor_tensor(G_lo[:], H_ps[0][:, 0:P], float(C) ** -0.5, G_hi[:].bitcast(f32),
                                           ALU.mult, ALU.subtract).then_inc(wlo_ready, 1)
            dve.wait_ge(s_VS, 16 * 2)
            W_copy(2)
            dve.wait_ge(up_ready, 1)
            dve.wait_ge(up_hi_ready, 1)
            nc.vector.tensor_tensor(up_lo[:], up[:], up_hi[:].bitcast(f32), ALU.subtract).then_inc(up_lo_ready, 1)
            dve.wait_ge(consts_ready, CONSTS)
            dve.wait_ge(A0_hi_ready, 1)
            A_rest().then_inc(A0_lo_ready, 1)
            dve.wait_ge(whi_ready, 2)
            nc.vector.tensor_tensor(WT_lo, H_ps[1][:, 0:2 * P].rearrange("p (n c) -> p n c", n=2), WT_hi.bitcast(f32),
                                    ALU.subtract).then_inc(wlo_ready, 1)
            w1_low(0, 1)
            row_max(0, 0)
            row_max(0, 1)
            for half in range(2):
                inv_sums(0, half)
                js = slice(half * ND // 2, (half + 1) * ND // 2)
                cols = slice(half * ND * PAIR // 2, (half + 1) * ND * PAIR // 2)
                pr = probs[:, js, :, :].rearrange("p j b m -> p (j b) m")
                dve.wait_ge(inv_sum_ready, half + 1)
                nc.vector.tensor_tensor(pr, pr, inv_sum[:, cols].unsqueeze(2).to_broadcast([P, ND * PAIR // 2, M]),
                                        ALU.mult).then_inc(probs_ready, 1)
            dve.wait_ge(AV_hi_ready, 1)
            v_rest(0).then_inc(AV_lo_ready, 1)
            PT_low_half(0, 0)
            w1_low(1, 2)
            PT_low_half(0, 1)
            dve.wait_ge(c1_hi_ready, 1)
            nc.vector.tensor_tensor(c1T_parts[:, :, :, 1, :], c1_turned_rep, c1T_parts[:, :, :, 0, :].bitcast(f32),
                                    ALU.subtract).then_inc(c1_lo_ready, 1)
            w1_low(2, 3)
            dve.wait_ge(tanh_ready, 2)
            x2_step(0)
            w1_low(3, 4)
            xf_step(0)
            w1_low(4, 5)
            xfT_low(0)
            w1_low(5, 10)
            t_low(0)
            w1_low(10, NF - W1_POOL)

            def body(t):
                first_tile = isinstance(t, int)
                choose(t, 0)
                mask(t, 0)
                if not first_tile:
                    result(t - 1)
                AV_low(t + 1)
                find_max(t, 1)
                hT_low(t, 0)
                row_max(t + 1, 0)
                row_max(t + 1, 1)
                scan(t, 1)
                mask(t, 1)
                inv_sums(t + 1, 0)
                find_max(t, 2)
                inv_sums(t + 1, 1)
                hT_low(t, 1)
                scan(t, 2)
                mask(t, 2)
                PT_low_half(t + 1, 0)
                find_max(t, 3)
                PT_low_half(t + 1, 1)
                scan(t, 3)
                hT_low(t, 2)
                mask(t, 3)
                x2_step(t + 1)
                xf_step(t + 1)
                hT_low(t, 3)
                xfT_low(t + 1)
                t_low(t + 1)

            body(0)
            with dve.Fori(1, TILES - 1) as t:
                body(t)
            t = TILES - 1
            choose(t, 0)
            result(t - 1)
            mask(t, 0)
            choose(t, 1)
            mask(t, 1)
            hT_low(t, 0)
            choose(t, 2)
            mask(t, 2)
            hT_low(t, 1)
            choose(t, 3)
            mask(t, 3)
            hT_low(t, 2)
            hT_low(t, 3)
            dve.wait_ge(ffn_done, TILES)
            for half in range(2):
                cs = slice(half * N // 2, (half + 1) * N // 2)
                nc.vector.scalar_tensor_tensor(rows[:, t, cs], ffn_ps[:, cs], tanh_g[:, 1:2], rows[:, t, cs],
                                               ALU.mult, ALU.add).then_inc(out_ready, 1)

        @block.tensor
        def _(pe):
            def AV(t):
                pe.wait_ge(ctx_lo_ready, t + 1)
                pe.wait_ge(x2_ready, t)
                nc.tensor.matmul(att_ps[0][:, 0:2 * M], G_hi[:], flat(ctx_parts[:]), start=True, stop=False)
                nc.tensor.matmul(att_ps[0][:, 0:M], G_lo[:], ctx_hi, start=False, stop=True)
                nc.tensor.matmul(v_ps(t), ctx_hi, flat(WT[:, 0, :, :]), start=True, stop=False)
                nc.tensor.matmul(v_ps(t)[:, 0:M], ctx_lo, WT_hi[:, 0, :], start=False, stop=True).then_inc(AV_done, 1)

            def energy(t):
                if isinstance(t, int) and t == 0:
                    pe.wait_ge(A0_lo_ready, 1)
                else:
                    pe.wait_ge(AV_lo_ready, t + 1)
                pe.wait_ge(up_lo_ready, t + 1)
                for j in range(ND):
                    js = slice(j * P, (j + 1) * P)
                    cs = slice(j % 2 * PAIR * M, (j % 2 + 1) * PAIR * M)
                    last = three_passes(att_ps[j // 2][:, cs], up_hi[:, js], up_lo[:, js], A_hi[:], A_lo[:])
                    if j % 2:
                        last.then_inc(energy_done, 1)

            def turn_probs(t):
                for half in range(2):
                    pe.wait_ge(probs_ready, t * 2 + half + 1)
                    for b in range(PAIR):
                        for jj in range(ND // 2):
                            at = (b * ND // 2 + jj) * P
                            last = nc.tensor.transpose(att_ps[half][:, at:at + P], probs[:, half * ND // 2 + jj, b, :], ident[:])
                    last.then_inc(probs_turned, 1)

            def xattn(t):
                pe.wait_ge(PT_lo_ready, t * 2 + 1)
                three_passes(att_ps[0][:], WT_hi[:, 1, :], WT_lo[:, 1, :], up_hi[:], up_lo[:], True, False)
                if isinstance(t, int) and t == 0:
                    pe.wait_ge(AV_lo_ready, 1)
                pe.wait_ge(PT_hi_ready, t * 2 + 2)
                for b in range(PAIR):
                    vs = slice(PAIR * b, PAIR * (b + 1))
                    nc.tensor.matmul(att_ps[0][:], flat(v_hi[:, vs, :]), PT_hi[:, :, b, :], start=False, stop=False)
                    nc.tensor.matmul(att_ps[0][:], flat(v_lo[:, vs, :]), PT_hi[:, :, b, :], start=False, stop=False)
                pe.wait_ge(PT_lo_ready, t * 2 + 2)
                for b in range(PAIR):
                    vs = slice(PAIR * b, PAIR * (b + 1))
                    last = nc.tensor.matmul(att_ps[0][:], flat(v_hi[:, vs, :]), PT_lo[:, :, b, :], start=False, stop=b == PAIR - 1)
                last.then_inc(xattn_done, 1)

            def turn_xf(t):
                pe.wait_ge(xf_ready, t + 1)
                for d in range(ND):
                    last = nc.tensor.transpose(xf_bank(t)[:, d * P:(d + 1) * P], xf[:, d * P:(d + 1) * P], ident[:])
                last.then_inc(xf_turned, 1)

            def low_rank(t):
                pe.wait_ge(xfT_lo_ready, t + 1)
                for d in range(ND):
                    last = nc.tensor.matmul(inter_ps[0][:, 0:2 * P], c1T_parts[:, d, :, :, :].rearrange("p a s r -> p (a s r)"),
                                            flat(xfT[:, d, :, :]), start=d == 0, stop=d == ND - 1)
                last.then_inc(t_done, 1)

            def inter(t, g):
                k0, n = GROUPS[g]
                if g == 0:
                    pe.wait_ge(t_lo_ready, t + 1)
                    pe.wait_ge(t_rest_ready, t + 1)
                if g >= 2:
                    pe.wait_ge(is_max_ready, t * NG + g - 1)
                nc.tensor.matmul(inter_ps[g % 2][:, 0:n * P], t_parts[:], c2T[:, k0 * P:(k0 + n) * P],
                                 start=True, stop=True).then_inc(inter_done, 1)

            def H(t, g, part=None):
                k0, n = GROUPS[g]
                fs = slice(k0 * P, (k0 + n) * P)
                ps = H_ps[g % 2][:, 0:n * P]
                if g >= 2:
                    pe.wait_ge(h_ready, t * NG + g - 1)
                if part != 1:
                    for d in range(ND):
                        nc.tensor.matmul(ps, xfT_hi[:, d, :], w1T_hi[:, d, fs], start=d == 0, stop=False)
                        nc.tensor.matmul(ps, xfT_hi[:, d, :], w1T_lo[:, d, fs], start=False, stop=False)
                if part != 0:
                    for d in range(ND):
                        last = nc.tensor.matmul(ps, xfT_lo[:, d, :], w1T_hi[:, d, fs], start=False, stop=d == ND - 1)
                    last.then_inc(H_done, 1)

            def turn_h(t, g):
                pe.wait_ge(h_ready, t * NG + g + 1)
                if g >= 1 and h_turn_bank(t, g) is h_turn_bank(t, g - 1):
                    pe.wait_ge(hT_lo_ready, t * NG + g)
                for k in range(GROUPS[g][1]):
                    ks = slice(k * P, (k + 1) * P)
                    last = nc.tensor.transpose(h_turn_bank(t, g)[:, ks], h[:, g % 2, ks], ident[:])
                last.then_inc(h_turned, 1)

            def down(t, g, a=0, b=3 * GF):
                k0, n = GROUPS[g]
                if a == 0:
                    pe.wait_ge(hT_lo_ready, t * NG + g + 1)
                    pe.wait_ge(w2_lo_ready, k0 + n)
                for i in range(a, min(b, 3 * n)):
                    k = i // 3
                    fs = slice(k * P, (k + 1) * P)
                    hT, w2 = ((hT_hi, w2_hi), (hT_hi, w2_lo), (hT_lo, w2_hi))[i % 3]
                    last = nc.tensor.matmul(ffn_ps[:], hT[:, g % 2, fs], w2[:, k0 + k, :], start=g == 0 and i == 0,
                                            stop=g == NG - 1 and i == 3 * n - 1)
                if g == NG - 1 and b >= 3 * n:
                    last.then_inc(ffn_done, 1)

            def turn_w1(k0, k1):
                for k in range(k0, k1):
                    slot = k % W1_SLOTS
                    pe.wait_ge(s_w1[slot], 16 * (k // W1_SLOTS + 1))
                    before = [j for j in range(k) if w1_banks[j] is w1_banks[k]]
                    if before:
                        pe.wait_ge(w1_lo_ready, before[-1] + 1)
                    for d in range(ND):
                        last = nc.tensor.transpose(w1_banks[k][:, d * P:(d + 1) * P], w1_stage[slot][:, d * P:(d + 1) * P], ident[:])
                    last.then_inc(w1_turned, 1)

            pe.wait_ge(ident_ready, 1)
            pe.wait_ge(W_bd_ready, 1)
            nc.tensor.matmul(H_ps[0][:, 0:P], W_bd[:, 0, :], W_bd[:, 1, :], start=True, stop=True).then_inc(wprod_ready, 1)
            pe.wait_ge(ctx_lo_ready, 1)
            pe.wait_ge(wlo_ready, 1)
            three_passes(att_ps[0][:, 0:M], G_hi[:], G_lo[:], ctx_hi, ctx_lo).then_inc(A0_done, 1)
            pe.wait_ge(W_bd_ready, 2)
            for n in range(2):
                last = nc.tensor.transpose(H_ps[1][:, n * P:(n + 1) * P], W_bd[:, 2 + n, :], ident[:])
            last.then_inc(wprod_ready, 1)
            turn_w1(0, 1)
            energy(0)
            pe.wait_ge(wlo_ready, 2)
            three_passes(v_ps(0)[:, 0:M], ctx_hi, ctx_lo, WT_hi[:, 0, :], WT_lo[:, 0, :]).then_inc(AV_done, 1)

            def turn_c1():
                pe.wait_ge(s_c1, 16)
                for d in range(ND):
                    last = nc.tensor.matmul(inter_ps[0][:, d * R:(d + 1) * R], c1_in[:, d * P:(d + 1) * P], ident[:, 0:R], start=True, stop=True)
                last.then_inc(c1_turned, 1)

            def turn_c2(g):
                k0, n = GROUPS[g]
                if g == 0:
                    pe.wait_ge(c2_parts_ready, 2)
                if g == 1:
                    pe.wait_ge(c1_lo_ready, 1)
                if g >= 2:
                    pe.wait_ge(c2_ready, g - 1)
                for k in range(n):
                    last = nc.tensor.transpose(inter_ps[1 - g % 2][:, k * P:(k + 1) * P],
                                               flat(c2_parts[:, k0 + k, :, :]).bitcast(f32), ident[:])
                last.then_inc(c2_turned, 1)

            turn_w1(1, 2)
            turn_c1()
            turn_w1(2, 4)
            turn_probs(0)
            turn_c2(0)
            xattn(0)
            turn_c2(1)
            turn_w1(4, 8)
            turn_c2(2)
            turn_c2(3)
            turn_xf(0)
            turn_w1(8, 9)
            pe.wait_ge(w1_lo_ready, GF)
            pe.wait_ge(xfT_hi_ready, 1)
            H(0, 0, 0)
            turn_w1(9, 10)
            pe.wait_ge(c2_ready, NG)
            low_rank(0)
            turn_w1(10, 12)
            H(0, 0, 1)

            def body(t):
                first_tile = isinstance(t, int)
                inter(t, 0)
                if first_tile:
                    turn_w1(12, NF)
                else:
                    H(t, 0)
                AV(t + 1)
                inter(t, 1)
                if first_tile:
                    pe.wait_ge(w1_lo_ready, 9)
                H(t, 1, 0)
                inter(t, 2)
                if first_tile:
                    pe.wait_ge(w1_lo_ready, NF - W1_POOL)
                    pe.wait_ge(w1_raw_ready, 1)
                turn_h(t, 0)
                H(t, 1, 1)
                if first_tile:
                    pe.wait_ge(w1_raw_ready, 2)
                energy(t + 1)
                down(t, 0)
                turn_h(t, 1)
                H(t, 2)
                turn_probs(t + 1)
                inter(t, 3)
                turn_h(t, 2)
                if first_tile:
                    pe.wait_ge(w1_pool_lo_ready, W1_POOL)
                H(t, 3)
                xattn(t + 1)
                down(t, 1)
                turn_h(t, 3)
                down(t, 2, 0, 4)
                turn_xf(t + 1)
                down(t, 2, 4)
                down(t, 3, 0, 1)
                low_rank(t + 1)
                down(t, 3, 1)

            body(0)
            with pe.Fori(1, TILES - 1) as t:
                body(t)
            t = TILES - 1
            inter(t, 0)
            inter(t, 1)
            H(t, 0)
            H(t, 1)
            turn_h(t, 0)
            inter(t, 2)
            H(t, 2)
            turn_h(t, 1)
            inter(t, 3)
            down(t, 0)
            H(t, 3)
            turn_h(t, 2)
            down(t, 1)
            turn_h(t, 3)
            down(t, 2)
            down(t, 3)


_INS = ['x', 'ctx_1024', 'g_xattn', 'g_ffn', 'L0_xattn_Wq', 'L0_xattn_Wk', 'L0_xattn_Wv', 'L0_xattn_Wskip',
        'L0_ffn_c1_w', 'L0_ffn_c2_w', 'L0_ffn_w1', 'L0_ffn_w2t']


def kernel(**inputs):
    import numpy as np
    import concourse.bacc as bacc
    from concourse.bass_utils import run_bass_kernel_spmd

    nc = bacc.Bacc("TRN2", target_bir_lowering=False, num_devices=1)
    arrays, args = {}, []
    for name in _INS:
        a = np.ascontiguousarray(inputs[name])
        arrays[f"in_{name}"] = a
        args.append(nc.dram_tensor(f"in_{name}", a.shape, mybir.dt.from_np(a.dtype), kind="ExternalInput").ap())
    x = arrays["in_x"]
    args.append(nc.dram_tensor("out", x.shape, mybir.dt.from_np(x.dtype), kind="ExternalOutput").ap())
    flamingo_gated_layer(nc, *args)
    r = run_bass_kernel_spmd(nc, [arrays], core_ids=[0])
    return r.results[0]["out"]
```
